# Optimizing a Trainium2 kernel written in Bass

```python
import numpy as np
import jax
import jax.numpy as jnp

def _softmax(x, axis=-1):
    return jax.nn.softmax(x, axis=axis)

def _gelu(x):
    return jax.nn.gelu(x, approximate=True)

def _silu(x):
    return jax.nn.silu(x)

def _sigmoid(x):
    return jax.nn.sigmoid(x)

def _layernorm(x, axis=-1, eps=1e-05):
    m = jnp.mean(x, axis=axis, keepdims=True)
    v = jnp.var(x, axis=axis, keepdims=True)
    return (x - m) / jnp.sqrt(v + eps)

def _scatter_add(tgt, idx, src, axis=0):
    return tgt.at[idx].add(src)

def _segment_sum(src, seg, n):
    return jax.ops.segment_sum(src, seg, n)
kernel_name = 'mk_gnn_resnorm_d2_gnn_r16_737259'

def setup_inputs(seed: int=0):
    np.random.seed(seed)
    _w = jnp.asarray

    def _rec_inputs():
        import jax
        import jax.numpy as jnp
        _gk = jax.random.key(seed)
        x = -0.0003929 + 0.9999 * jax.random.normal(jax.random.fold_in(_gk, 1), (8192, 128), jnp.float32)
        src = jax.random.randint(jax.random.fold_in(_gk, 2), (262144,), 0, 8192, jnp.int32)
        dst = jnp.minimum((8192 * jax.random.uniform(jax.random.fold_in(_gk, 3), (262144,)) ** 2.0).astype(jnp.int32), 131071)
        _o = jnp.argsort(dst, stable=True)
        src = src[_o]
        dst = dst[_o]
        edge_attr_9 = 0.000458729 + 1.00015 * jax.random.normal(jax.random.fold_in(_gk, 12), (262144, 9), jnp.float32)
        edge_weight = jax.random.uniform(jax.random.fold_in(_gk, 14), (262144,), jnp.float32, 0.0, 1)
        return (x, src, dst, edge_attr_9, edge_weight)
    x, src, dst, edge_attr_9, edge_weight = _rec_inputs()

    def _L0_gnn_setup():
        import jax, jax.numpy as jnp
        import numpy as np
        N = 8192
        E = 262144
        D = 128
        key = jax.random.key(seed)
        k1, k2, k3, k4, k5 = jax.random.split(key, 5)
        x = jax.random.normal(k1, (N, D), dtype=jnp.float32)
        edge_row = jax.random.randint(k2, (E,), 0, N, dtype=jnp.int32)
        edge_col = jax.random.randint(k3, (E,), 0, N, dtype=jnp.int32)
        edge_vals = jax.random.uniform(k4, (E,), dtype=jnp.float32)
        W = jax.random.normal(k5, (D, D), dtype=jnp.float32) * (1.0 / np.sqrt(D))
        return {'x': x, 'edge_row': edge_row, 'edge_col': edge_col, 'edge_vals': edge_vals, 'W': W}
    _L0_gnn_all = _L0_gnn_setup()
    _L0_gnn_in = {k: v for k, v in _L0_gnn_all.items() if k in ('W',)}
    del _L0_gnn_all

    def _L1_gnn_setup():
        import jax, jax.numpy as jnp
        import numpy as np
        from fractions import Fraction
        from math import factorial

        def _su2_cg_coeff(j1, m1, j2, m2, j3, m3):
            if m3 != m1 + m2:
                return 0.0
            vmin = int(max(-j1 + j2 + m3, -j1 + m1, 0))
            vmax = int(min(j2 + j3 + m1, j3 - j1 + j2, j3 + m3))
            f = lambda n: factorial(round(n))
            C = ((2.0 * j3 + 1.0) * Fraction(f(j3 + j1 - j2) * f(j3 - j1 + j2) * f(j1 + j2 - j3) * f(j3 + m3) * f(j3 - m3), f(j1 + j2 + j3 + 1) * f(j1 - m1) * f(j1 + m1) * f(j2 - m2) * f(j2 + m2))) ** 0.5
            S = 0
            for v in range(vmin, vmax + 1):
                S += (-1) ** (v + j2 + m2) * Fraction(f(j2 + j3 + m1 - v) * f(j1 - m1 + v), f(v) * f(j3 - j1 + j2 - v) * f(j3 + m3 - v) * f(v + j1 - j2 - m3))
            return float(C * S)

        def _change_basis_real_to_complex(l):
            q = np.zeros((2 * l + 1, 2 * l + 1), dtype=np.complex128)
            for m in range(-l, 0):
                q[l + m, l + abs(m)] = 1 / np.sqrt(2)
                q[l + m, l - abs(m)] = -1j / np.sqrt(2)
            q[l, l] = 1
            for m in range(1, l + 1):
                q[l + m, l + abs(m)] = (-1) ** m / np.sqrt(2)
                q[l + m, l - abs(m)] = 1j * (-1) ** m / np.sqrt(2)
            return (-1j) ** l * q

        def wigner_3j(l1, l2, l3):
            C = np.zeros((2 * l1 + 1, 2 * l2 + 1, 2 * l3 + 1))
            for m1 in range(-l1, l1 + 1):
                for m2 in range(-l2, l2 + 1):
                    m3 = m1 + m2
                    if abs(m3) <= l3:
                        C[l1 + m1, l2 + m2, l3 + m3] = _su2_cg_coeff(l1, m1, l2, m2, l3, m3)
            Q1 = _change_basis_real_to_complex(l1)
            Q2 = _change_basis_real_to_complex(l2)
            Q3 = _change_basis_real_to_complex(l3)
            Cc = np.einsum('ij,kl,mn,ikn->jlm', Q1, Q2, np.conj(Q3.T), C.astype(np.complex128))
            Cr = np.real(Cc)
            return Cr / np.linalg.norm(Cr)
        MUL = 32
        IRREPS_IN = [(MUL, 0, 1), (MUL, 1, -1)]
        IRREPS_SH = [(1, 0, 1), (1, 1, -1), (1, 2, 1)]
        IRREPS_OUT = [(MUL, 0, 1), (MUL, 1, -1)]
        NUM_NEIGHBORS = 10.0
        N_NODES, N_EDGES = (625, 6250)

        def _dim(irreps):
            return sum((m * (2 * l + 1) for m, l, _ in irreps))

        def _slices(irreps):
            s, out = (0, [])
            for m, l, _ in irreps:
                d = m * (2 * l + 1)
                out.append((s, s + d))
                s += d
            return out

        def _instructions():
            ins = []
            for i1, (m1, l1, p1) in enumerate(IRREPS_IN):
                for i2, (m2, l2, p2) in enumerate(IRREPS_SH):
                    for io, (mo, lo, po) in enumerate(IRREPS_OUT):
                        if abs(l1 - l2) <= lo <= l1 + l2 and p1 * p2 == po:
                            ins.append((i1, i2, io))
            return ins
        _INSTR = _instructions()
        _SL_IN, _SL_SH, _SL_OUT = (_slices(IRREPS_IN), _slices(IRREPS_SH), _slices(IRREPS_OUT))
        _W3J = [jnp.asarray(wigner_3j(IRREPS_IN[i1][1], IRREPS_SH[i2][1], IRREPS_OUT[io][1]), dtype=jnp.float32) for i1, i2, io in _INSTR]
        _NORM = []
        for _i1, _i2, _io in _INSTR:
            _alpha = 2 * IRREPS_OUT[_io][1] + 1
            _x = sum((IRREPS_IN[j1][0] * IRREPS_SH[j2][0] for j1, j2, jo in _INSTR if jo == _io))
            _NORM.append(float(np.sqrt(_alpha / _x)))

        def _tensor_product(x1, x2, weights):
            E = x1.shape[0]
            out = jnp.zeros((E, _dim(IRREPS_OUT)), dtype=x1.dtype)
            for k, (i1, i2, io) in enumerate(_INSTR):
                m1, l1, _ = IRREPS_IN[i1]
                m2, l2, _ = IRREPS_SH[i2]
                mo, lo, _ = IRREPS_OUT[io]
                a, b = _SL_IN[i1]
                c, d = _SL_SH[i2]
                e, f = _SL_OUT[io]
                x1s = x1[:, a:b].reshape(E, m1, 2 * l1 + 1)
                x2s = x2[:, c:d].reshape(E, m2, 2 * l2 + 1)
                seg = jnp.einsum('uvw,ijk,eui,evj->ewk', weights[k], _W3J[k], x1s, x2s, optimize='optimal') * _NORM[k]
                out = out.at[:, e:f].add(seg.reshape(E, mo * (2 * lo + 1)))
            return out
        key = jax.random.key(seed)
        ks = jax.random.split(key, 8)
        x = jax.random.normal(ks[0], (N_NODES, _dim(IRREPS_IN)), dtype=jnp.float32)
        edge_index = jax.random.randint(ks[1], (2, N_EDGES), 0, N_NODES)
        edge_attr = jax.random.normal(ks[2], (N_EDGES, _dim(IRREPS_SH)), dtype=jnp.float32)
        ws = {f'w{k}': jax.random.normal(ks[3 + k], (MUL, 1, MUL), dtype=jnp.float32) for k in range(len(_INSTR))}
        return {'x': x, 'edge_index': edge_index, 'edge_attr': edge_attr, **ws}
    _L1_gnn_all = _L1_gnn_setup()
    _L1_gnn_in = {k: v for k, v in _L1_gnn_all.items() if k in ('w0', 'w1', 'w2', 'w3', 'w4')}
    del _L1_gnn_all
    return {'x': x, 'src': src, 'dst': dst, 'edge_attr_9': edge_attr_9, 'edge_weight': edge_weight, 'L0_gnn_W': _L0_gnn_in['W'], 'L1_gnn_w0': _L1_gnn_in['w0'], 'L1_gnn_w1': _L1_gnn_in['w1'], 'L1_gnn_w2': _L1_gnn_in['w2'], 'L1_gnn_w3': _L1_gnn_in['w3'], 'L1_gnn_w4': _L1_gnn_in['w4']}

def reference(x, src, dst, edge_attr_9, edge_weight, L0_gnn_W, L1_gnn_w0, L1_gnn_w1, L1_gnn_w2, L1_gnn_w3, L1_gnn_w4):
    import jax
    import jax.numpy as jnp

    def _L0_gnn_ref(x, edge_row, edge_col, edge_vals, W):
        import jax, jax.numpy as jnp
        import numpy as np
        N = 8192
        E = 262144
        D = 128
        gathered = x[edge_col] * edge_vals[:, None]
        pre_embed = jax.ops.segment_sum(gathered, edge_row, num_segments=N)
        return pre_embed @ W.T

    def _L1_gnn_ref(x, edge_index, edge_attr, w0, w1, w2, w3, w4):
        import jax, jax.numpy as jnp
        import numpy as np
        from fractions import Fraction
        from math import factorial

        def _su2_cg_coeff(j1, m1, j2, m2, j3, m3):
            if m3 != m1 + m2:
                return 0.0
            vmin = int(max(-j1 + j2 + m3, -j1 + m1, 0))
            vmax = int(min(j2 + j3 + m1, j3 - j1 + j2, j3 + m3))
            f = lambda n: factorial(round(n))
            C = ((2.0 * j3 + 1.0) * Fraction(f(j3 + j1 - j2) * f(j3 - j1 + j2) * f(j1 + j2 - j3) * f(j3 + m3) * f(j3 - m3), f(j1 + j2 + j3 + 1) * f(j1 - m1) * f(j1 + m1) * f(j2 - m2) * f(j2 + m2))) ** 0.5
            S = 0
            for v in range(vmin, vmax + 1):
                S += (-1) ** (v + j2 + m2) * Fraction(f(j2 + j3 + m1 - v) * f(j1 - m1 + v), f(v) * f(j3 - j1 + j2 - v) * f(j3 + m3 - v) * f(v + j1 - j2 - m3))
            return float(C * S)

        def _change_basis_real_to_complex(l):
            q = np.zeros((2 * l + 1, 2 * l + 1), dtype=np.complex128)
            for m in range(-l, 0):
                q[l + m, l + abs(m)] = 1 / np.sqrt(2)
                q[l + m, l - abs(m)] = -1j / np.sqrt(2)
            q[l, l] = 1
            for m in range(1, l + 1):
                q[l + m, l + abs(m)] = (-1) ** m / np.sqrt(2)
                q[l + m, l - abs(m)] = 1j * (-1) ** m / np.sqrt(2)
            return (-1j) ** l * q

        def wigner_3j(l1, l2, l3):
            C = np.zeros((2 * l1 + 1, 2 * l2 + 1, 2 * l3 + 1))
            for m1 in range(-l1, l1 + 1):
                for m2 in range(-l2, l2 + 1):
                    m3 = m1 + m2
                    if abs(m3) <= l3:
                        C[l1 + m1, l2 + m2, l3 + m3] = _su2_cg_coeff(l1, m1, l2, m2, l3, m3)
            Q1 = _change_basis_real_to_complex(l1)
            Q2 = _change_basis_real_to_complex(l2)
            Q3 = _change_basis_real_to_complex(l3)
            Cc = np.einsum('ij,kl,mn,ikn->jlm', Q1, Q2, np.conj(Q3.T), C.astype(np.complex128))
            Cr = np.real(Cc)
            return Cr / np.linalg.norm(Cr)
        MUL = 32
        IRREPS_IN = [(MUL, 0, 1), (MUL, 1, -1)]
        IRREPS_SH = [(1, 0, 1), (1, 1, -1), (1, 2, 1)]
        IRREPS_OUT = [(MUL, 0, 1), (MUL, 1, -1)]
        NUM_NEIGHBORS = 10.0
        N_NODES, N_EDGES = (625, 6250)

        def _dim(irreps):
            return sum((m * (2 * l + 1) for m, l, _ in irreps))

        def _slices(irreps):
            s, out = (0, [])
            for m, l, _ in irreps:
                d = m * (2 * l + 1)
                out.append((s, s + d))
                s += d
            return out

        def _instructions():
            ins = []
            for i1, (m1, l1, p1) in enumerate(IRREPS_IN):
                for i2, (m2, l2, p2) in enumerate(IRREPS_SH):
                    for io, (mo, lo, po) in enumerate(IRREPS_OUT):
                        if abs(l1 - l2) <= lo <= l1 + l2 and p1 * p2 == po:
                            ins.append((i1, i2, io))
            return ins
        _INSTR = _instructions()
        _SL_IN, _SL_SH, _SL_OUT = (_slices(IRREPS_IN), _slices(IRREPS_SH), _slices(IRREPS_OUT))
        _W3J = [jnp.asarray(wigner_3j(IRREPS_IN[i1][1], IRREPS_SH[i2][1], IRREPS_OUT[io][1]), dtype=jnp.float32) for i1, i2, io in _INSTR]
        _NORM = []
        for _i1, _i2, _io in _INSTR:
            _alpha = 2 * IRREPS_OUT[_io][1] + 1
            _x = sum((IRREPS_IN[j1][0] * IRREPS_SH[j2][0] for j1, j2, jo in _INSTR if jo == _io))
            _NORM.append(float(np.sqrt(_alpha / _x)))

        def _tensor_product(x1, x2, weights):
            E = x1.shape[0]
            out = jnp.zeros((E, _dim(IRREPS_OUT)), dtype=x1.dtype)
            for k, (i1, i2, io) in enumerate(_INSTR):
                m1, l1, _ = IRREPS_IN[i1]
                m2, l2, _ = IRREPS_SH[i2]
                mo, lo, _ = IRREPS_OUT[io]
                a, b = _SL_IN[i1]
                c, d = _SL_SH[i2]
                e, f = _SL_OUT[io]
                x1s = x1[:, a:b].reshape(E, m1, 2 * l1 + 1)
                x2s = x2[:, c:d].reshape(E, m2, 2 * l2 + 1)
                seg = jnp.einsum('uvw,ijk,eui,evj->ewk', weights[k], _W3J[k], x1s, x2s, optimize='optimal') * _NORM[k]
                out = out.at[:, e:f].add(seg.reshape(E, mo * (2 * lo + 1)))
            return out
        i, j = (edge_index[0], edge_index[1])
        summand = _tensor_product(x[i], edge_attr, [w0, w1, w2, w3, w4])
        out = jax.ops.segment_sum(summand, j, num_segments=x.shape[0])
        return out / float(np.sqrt(NUM_NEIGHBORS))
    edge_index = jnp.stack([src, dst])
    x = _layernorm(x + _L0_gnn_ref(x, src, dst, edge_weight, L0_gnn_W), axis=-1)
    x = _layernorm(x + _L1_gnn_ref(x, edge_index, edge_attr_9, L1_gnn_w0, L1_gnn_w1, L1_gnn_w2, L1_gnn_w3, L1_gnn_w4), axis=-1)
    return x

_drawn_inputs = setup_inputs


def setup_inputs(seed=0):
    import zlib

    import numpy as np

    out = dict(_drawn_inputs(seed))
    spreads = {}
    factors = {}
    for name, (base, spread) in spreads.items():
        noise = np.random.default_rng([zlib.crc32(name.encode()), seed]).standard_normal(out[name].shape)
        drawn = base * np.exp(spread * noise) if base else spread * noise
        out[name] = jnp.asarray(drawn.astype(out[name].dtype))
    for name, factor in factors.items():
        out[name] = (out[name] * factor).astype(out[name].dtype)
    return out
```

```python
from contextlib import ExitStack

import numpy as np

import concourse.bass as bass
from concourse import mybir

ALU = mybir.AluOpType
ACT = mybir.ActivationFunctionType
AX_X = mybir.AxisListType.X
F32 = mybir.dt.float32
BF16 = mybir.dt.bfloat16
I32 = mybir.dt.int32

P = 128
D = 128
MUL = 32
NA = 9
ROW_TILES = 16
HALF_TILES = 8
QUAD_TILES = 4
ROW_EDGES = ROW_TILES * P
TABLES = 4
EPS = 1e-5
NEIGHBORS = 10.0

WIN0 = 128
WIN = 16
QUAD_WIN = 56
GROUP_WIN = 192

C_IDENT = 0
C_COEF = C_IDENT + P
C_DUPW = C_COEF + 4 * NA
C_DUPT = C_DUPW + 2
C_IOTA = C_DUPT + 2
C_PID = C_IOTA + WIN
C_SPARE = C_PID + 1
C_ALL = C_SPARE + 1


def wigner_121():
    c = np.zeros((3, 5, 3))
    c[0, 0, 2] = c[2, 0, 0] = 1.0
    c[0, 1, 1] = c[1, 1, 0] = 1.0
    c[0, 2, 0] = c[2, 2, 2] = -1.0 / np.sqrt(3.0)
    c[1, 2, 1] = 2.0 / np.sqrt(3.0)
    c[1, 3, 2] = c[2, 3, 1] = 1.0
    c[0, 4, 0] = -1.0
    c[2, 4, 2] = 1.0
    return c / np.sqrt(10.0)


def constants(n_nodes):
    c = np.zeros((P, C_ALL), np.float64)
    p = np.arange(P)
    c[:, C_IDENT:C_IDENT + P] = np.eye(P)
    coef = np.zeros((P, NA, 4))
    to_scalar = np.sqrt(1.0 / (2 * MUL)) / np.sqrt(NEIGHBORS)
    to_vector = np.sqrt(3.0 / (3 * MUL)) / np.sqrt(NEIGHBORS)
    dot = 1.0 / np.sqrt(3.0)
    i = np.arange(P - MUL) % 3
    coef[:MUL, 0, 0] = to_scalar
    coef[MUL:, 0, 1:] = np.eye(3)[i] * dot * to_vector
    for j in range(3):
        coef[:MUL, 1 + j, 1 + j] = dot * to_vector
        coef[MUL:, 1 + j, 0] = (i == j) * dot * to_scalar
    for j in range(5):
        coef[MUL:, 4 + j, 1:] = wigner_121()[i, j] * to_vector
    c[:, C_COEF:C_COEF + 4 * NA] = coef.reshape(P, -1)
    half = P // 2
    w = 2.0 ** (126 - 2 * (p % half))
    c[:half, C_DUPW] = w[:half]
    c[half:, C_DUPW + 1] = w[half:]
    c[:half, C_DUPT] = 2 * w[:half]
    c[:half, C_DUPT + 1] = 3e38
    c[half:, C_DUPT] = 0.5
    c[half:, C_DUPT + 1] = 2 * w[half:]
    c[:, C_IOTA:C_IOTA + WIN] = np.arange(WIN)
    c[:, C_PID] = p
    c[:, C_SPARE] = n_nodes + p
    return c.astype(np.float32)


class Shared:
    pass


def gnn_kernel(nc, x, src, dst, attr, weight, w_lin, w_tp, consts, out, tables, x1):
    g = Shared()
    g.N = x.shape[0]
    g.E = src.shape[0]
    g.RN = g.E // ROW_EDGES
    g.TN = g.E // P
    g.PASSES0 = g.N // WIN0
    g.PASSES1 = g.N // WIN
    assert g.E % (2 * ROW_EDGES) == 0 and g.RN <= P and g.N % 1024 == 0
    with ExitStack() as ctx:
        def sb(name, shape, dt):
            return ctx.enter_context(nc.sbuf_tensor(name, shape, dt))

        g.cst = sb("cst", [P, C_ALL], F32)
        g.ident_bf = sb("ident_bf", [P, g.RN + 1], BF16)
        g.acc = sb("acc", [P, g.N + GROUP_WIN], F32)
        g.src_col = sb("src_col", [P, g.TN + ROW_TILES], F32)
        g.dst_col = sb("dst_col", [P, g.TN], F32)
        g.tile_start = sb("tile_start", [P, g.TN], F32)
        g.attr_col = sb("attr_col", [P, g.TN, NA], F32)
        g.keep = sb("keep", [P, 2], F32)
        g.jump = sb("jump", [P, 2], F32)
        g.n_pass = sb("n_pass", [P, 2], I32)
        g.w_t = sb("w_t", [P, D], F32)
        with ExitStack() as mid:
            def sm(name, shape, dt):
                return mid.enter_context(nc.sbuf_tensor(name, shape, dt))
            g.w_col = sm("w_col", [P, g.TN], F32)
            g.half_start = sm("half_start", [P, g.RN, 2], F32)
            g.hi_lo = [[sm(f"{n}_{h}", [P, ROW_EDGES], BF16) for h in ("hi", "lo")] for n in ("src", "dst")]
            setup(nc, g, src, dst, attr, weight, w_lin, consts, tables)
            layer0(nc, g, x, tables)
        norm_stage(nc, g, "norm0", x, x1, tables)
        layer1(nc, g, x1, w_tp)
        norm_stage(nc, g, "norm1", x1, out, None)


def setup(nc, g, src, dst, attr, weight, w_lin, consts, tables):
    RN, TN = g.RN, g.TN
    with ExitStack() as ctx:
        def sb(name, shape, dt):
            return ctx.enter_context(nc.sbuf_tensor(name, shape, dt))

        def sem(name):
            return ctx.enter_context(nc.semaphore(name))

        rows_i = [sb(f"rows_i{i}", [P, ROW_EDGES], I32) for i in range(2)]
        rows_f = [sb(f"rows_f{i}", [P, ROW_EDGES], F32) for i in range(3)]
        chunk = [sb(f"chunk{i}", [P, P * NA], F32) for i in range(2)]
        w_in = sb("w_in", [P, D], F32)
        ones = sb("ones", [P, P], F32)
        miss = sb("miss", [P, 4], F32)
        reach = sb("reach", [P, 4], F32)
        some = sb("some", [P, 2], F32)
        pt = ctx.enter_context(nc.psum_tensor("pt", [P, 4, 512], F32))
        pa = ctx.enter_context(nc.psum_tensor("pa", [P, 4, 512], F32))

        consts_in = sem("consts_in")
        rows_in = [sem(f"rows_in{i}") for i in range(3)]
        chunk_in = [sem(f"chunk_in{i}") for i in range(2)]
        zeroed = sem("zeroed")
        filled = sem("filled")
        rows_made = sem("rows_made")
        ident_made = sem("ident_made")
        split_made = sem("split_made")
        group_done = sem("group_done")
        group_out = sem("group_out")
        attr_done = sem("attr_done")
        attr_out = sem("attr_out")
        miss_made = sem("miss_made")
        miss_sum = sem("miss_sum")
        dve_step = sem("dve_step")
        wt_done = sem("wt_done")

        col_groups = [(which, q) for q in range(4) for which in range(3)]
        n_groups = len(col_groups) + 4
        attr_rows = attr.rearrange("(r k e) m -> r k (e m)", k=ROW_TILES, e=P)
        block = ctx.enter_context(nc.Block())

        @block.sync
        def _(sp):
            sp.dma_start(g.cst[:], consts).then_inc(consts_in, 16)
            sp.dma_start(w_in[:], w_lin).then_inc(consts_in, 16)
            sp.dma_start(rows_i[0][0:RN, :], src.rearrange("(r c) -> r c", r=RN)).then_inc(rows_in[0], 16)
            sp.dma_start(rows_i[1][0:RN, :], dst.rearrange("(r c) -> r c", r=RN)).then_inc(rows_in[1], 16)
            sp.dma_start(rows_f[2][0:RN, :], weight.rearrange("(r c) -> r c", r=RN)).then_inc(rows_in[2], 16)
            for k in range(ROW_TILES):
                if k >= 2:
                    sp.wait_ge(attr_done, k - 1)
                sp.dma_start(chunk[k % 2][0:RN, :], attr_rows[:, k]).then_inc(chunk_in[k % 2], 16)

        @block.gpsimd
        def _(pool):
            pool.wait_ge(zeroed, 1)
            for k in range(TABLES):
                pool.dma_start(tables[k].rearrange("(p a) d -> p (a d)", p=P),
                               g.acc[:, 0:g.N + P]).then_inc(filled, 16)
            pool.wait_ge(filled, 16 * TABLES)

        @block.vector
        def _(dve):
            steps = [0]

            def link(ins):
                steps[0] += 1
                ins.then_inc(dve_step, 1)
                dve.wait_ge(dve_step, steps[0])

            nc.vector.memset(g.acc[:], 0.0).then_inc(zeroed, 1)
            nc.vector.memset(ones[:], 1.0)
            dve.wait_ge(consts_in, 32)
            nc.vector.tensor_copy(g.ident_bf[:, 0:RN], g.cst[:, C_IDENT:C_IDENT + RN])
            nc.vector.tensor_copy(g.ident_bf[:, RN:RN + 1], g.cst[:, C_IDENT:C_IDENT + 1]).then_inc(ident_made, 1)
            for i in range(2):
                dve.wait_ge(rows_in[i], 16)
                nc.vector.tensor_copy(rows_f[i][0:RN, :], rows_i[i][0:RN, :]).then_inc(rows_made, 1)
            dve.wait_ge(rows_made, 2)
            for i in (1, 0):
                hi, lo = g.hi_lo[i]
                link(nc.vector.tensor_scalar(rows_i[i][0:RN, :], rows_i[i][0:RN, :], P - 1, None, ALU.bitwise_and))
                link(nc.vector.tensor_copy(lo[0:RN, :], rows_i[i][0:RN, :]))
                nc.vector.tensor_tensor(hi[0:RN, :], rows_f[i][0:RN, :], rows_i[i][0:RN, :],
                                        ALU.subtract).then_inc(split_made, 1)
            dve.wait_ge(group_out, n_groups)
            nc.vector.tensor_copy(g.src_col[:, TN:TN + ROW_TILES], g.src_col[:, 0:ROW_TILES])
            starts = g.tile_start[:].rearrange("p (s t) -> p s t", t=HALF_TILES)
            halves = g.half_start[:].rearrange("p r h -> p (r h)")
            link(nc.vector.tensor_scalar(halves, starts[:, :, 0], float(g.N - WIN0), None, ALU.min))
            far = rows_f[0]
            dve.wait_ge(split_made, 2)

            def farthest(col, a, b, shape, limit):
                n = shape[0] * shape[1]
                v = far[:, 0:n].rearrange("p (a b) -> p a b", b=shape[1])
                link(nc.vector.scalar_tensor_tensor(out=v, in0=a, scalar=-limit / 2.0, in1=b, op0=ALU.add,
                                                    op1=ALU.subtract))
                link(nc.vector.tensor_reduce(reach[:, col:col + 1], far[:, 0:n], AX_X, ALU.max,
                                             apply_absolute_value=True))
                link(nc.vector.tensor_scalar(miss[:, col:col + 1], reach[:, col:col + 1], limit / 2.0, None,
                                             ALU.is_gt))

            H, Q, R = HALF_TILES, QUAD_TILES, ROW_TILES
            s8 = [P, TN // H, H]
            s4 = [P, TN // Q, Q]
            farthest(0, g.dst_col[:].rearrange("p (a b) -> p a b", b=H), halves.unsqueeze(2).to_broadcast(s8),
                     s8[1:], WIN0 - 1.0)
            farthest(1, g.dst_col[:].rearrange("p (a b) -> p a b", b=H), starts, s8[1:], WIN - 1.0)
            quads = g.tile_start[:].rearrange("p (a b) -> p a b", b=Q)
            farthest(2, quads, quads[:, :, 0:1].to_broadcast(s4), s4[1:], float(QUAD_WIN - WIN))
            q_in_row = g.tile_start[:].rearrange("p (a b c) -> p a b c", b=R // Q, c=Q)[:, :, :, 0]
            farthest(3, q_in_row, q_in_row[:, :, 0:1].to_broadcast([P, RN, R // Q]), [RN, R // Q],
                     float(GROUP_WIN - QUAD_WIN))
            nc.vector.tensor_tensor(miss[:, 1:2], miss[:, 1:2], miss[:, 2:3], ALU.max).then_inc(dve_step, 1)
            steps[0] += 1
            dve.wait_ge(dve_step, steps[0])
            nc.vector.tensor_tensor(miss[:, 1:2], miss[:, 1:2], miss[:, 3:4], ALU.max).then_inc(miss_made, 1)
            dve.wait_ge(miss_sum, 1)
            link(nc.vector.tensor_scalar(some[:], pa[:, 0, 0:2], 0.5, None, ALU.is_gt))
            nc.vector.tensor_scalar(g.keep[:], some[:], -1.0, 1.0, ALU.mult, ALU.add)
            for l, (win, passes) in enumerate(((WIN0, g.PASSES0), (WIN, g.PASSES1))):
                nc.vector.tensor_scalar(g.jump[:, l:l + 1], some[:, l:l + 1], float(win), None, ALU.mult)
                nc.vector.tensor_scalar(g.n_pass[:, l:l + 1], some[:, l:l + 1], float(passes - 1), 1.0,
                                        ALU.mult, ALU.add)

        @block.tensor
        def _(pe):
            ident = g.cst[:, C_IDENT:C_IDENT + P]
            ident_rows = g.cst[0:RN, C_IDENT:C_IDENT + RN]
            pe.wait_ge(consts_in, 32)
            n = 0
            for which, q in col_groups:
                if which < 2:
                    pe.wait_ge(rows_made, which + 1)
                else:
                    pe.wait_ge(rows_in[2], 16)
                if n >= 4:
                    pe.wait_ge(group_out, n - 3)
                for j in range(4):
                    k = 4 * q + j
                    last = nc.tensor.transpose(pt[:, n % 4, j * P:j * P + RN],
                                               rows_f[which][0:RN, k * P:(k + 1) * P], ident_rows)
                last.then_inc(group_done, 1)
                n += 1
            pe.wait_ge(ident_made, 1)
            pe.wait_ge(split_made, 1)
            for q in range(4):
                pe.wait_ge(group_out, n - 3)
                for j in range(4):
                    k = 4 * q + j
                    for part in range(2):
                        first = g.hi_lo[1][part][0:RN, k * P:k * P + 1].to_broadcast([RN, P])
                        last = nc.tensor.matmul(pt[:, n % 4, j * P:j * P + RN], first, g.ident_bf[0:RN, 0:RN],
                                                start=(part == 0), stop=(part == 1))
                last.then_inc(group_done, 1)
                n += 1
            for k in range(ROW_TILES):
                pe.wait_ge(chunk_in[k % 2], 16 * (k // 2 + 1))
                if k >= 1:
                    pe.wait_ge(attr_out, k)
                edges = chunk[k % 2][0:RN, :].rearrange("r (e m) -> r e m", m=NA)
                for m in range(NA):
                    last = nc.tensor.transpose(pa[:, m // 3, (m % 3) * P:(m % 3) * P + RN], edges[:, :, m],
                                               ident_rows)
                last.then_inc(attr_done, 1)
            pe.wait_ge(attr_out, ROW_TILES)
            nc.tensor.transpose(pa[:, 3, 0:P], w_in[:], ident).then_inc(wt_done, 1)
            pe.wait_ge(miss_made, 1)
            nc.tensor.matmul(pa[:, 0, 0:4], ones[:], miss[:], start=True, stop=True).then_inc(miss_sum, 1)

        @block.scalar
        def _(act):
            cols = [g.src_col, g.dst_col, g.w_col]
            for n in range(n_groups):
                if n < len(col_groups):
                    which, q = col_groups[n]
                    dest = cols[which]
                else:
                    q, dest = n - len(col_groups), g.tile_start
                act.wait_ge(group_done, n + 1)
                o = dest[:, 0:TN].rearrange("p (r k) -> p k r", k=ROW_TILES)[:, 4 * q:4 * q + 4, :]
                i = pt[:, n % 4, :].rearrange("p (j r) -> p j r", j=4)[:, :, 0:RN]
                nc.scalar.copy(o, i).then_inc(group_out, 1)
            to = g.attr_col[:].rearrange("p (r k) m -> p k r m", k=ROW_TILES)
            for k in range(ROW_TILES):
                act.wait_ge(attr_done, k + 1)
                for b in range(3):
                    last = nc.scalar.copy(to[:, k, :, 3 * b:3 * b + 3],
                                          pa[:, b, 0:3 * P].rearrange("p (m r) -> p r m", m=3)[:, 0:RN, :])
                last.then_inc(attr_out, 1)
            act.wait_ge(wt_done, 1)
            nc.scalar.copy(g.w_t[:], pa[:, 3, 0:P])


def layer0(nc, g, x, tables):
    RN = g.RN
    H = HALF_TILES
    R_COLS = D + 2
    with ExitStack() as ctx:
        def sb(name, shape, dt):
            return ctx.enter_context(nc.sbuf_tensor(name, shape, dt))

        def sem(name):
            return ctx.enter_context(nc.semaphore(name))

        node_id = sb("node_id", [P, RN * 2], F32)
        start_i = sb("start_i", [P, RN * 2], I32)
        moved = sb("moved", [P, 2], F32)
        win_x = [sb(f"win_x{i}", [P, D], F32) for i in range(2)]
        win_r = [sb(f"win_r{i}", [P, D], F32) for i in range(2)]
        win_s = [sb(f"win_s{i}", [P, 3, D], BF16) for i in range(2)]
        onehot = [sb(f"onehot{i}", [P, H * P], BF16) for i in range(2)]
        same = [sb(f"same{i}", [P, H, P], F32) for i in range(2)]
        msg = [sb(f"msg{i}", [P, H, R_COLS], F32) for i in range(2)]
        sums = sb("sums", [P, 2 * H, R_COLS], F32)
        row_no = sb("row_no", [P, 2 * H], I32)
        first2 = sb("first2", [P, H, 2], F32)
        first = sb("first", [P, H], F32)
        away = sb("away", [P, H], F32)
        dst_b = ctx.enter_context(nc.psum_tensor("dst_b", [P, H * P], F32))
        src_b = ctx.enter_context(nc.psum_tensor("src_b", [P, H * P], F32))
        got = ctx.enter_context(nc.psum_tensor("got", [P, 2, 512], F32))
        added = ctx.enter_context(nc.psum_tensor("added", [P, 2, 512], F32))

        tables_made = sem("l0_tables_made")
        win_in = [sem(f"win_in{i}") for i in range(2)]
        win_split = sem("win_split")
        ids_shown = sem("ids_shown")
        onehot_made = sem("onehot_made")
        same_made = sem("same_made")
        fetched = sem("fetched")
        msgs_made = sem("msgs_made")
        summed = sem("summed")
        sums_out = sem("sums_out")
        rows_known = sem("rows_known")
        turns = sem("turns")
        table_add = [sem(f"table_add{k}") for k in range(TABLES)]
        msg_init = sem("msg_init")
        dve_step = sem("l0_dve_step")
        part_made = sem("part_made")
        row_step = sem("row_step")
        block = ctx.enter_context(nc.Block())

        def passes(eng):
            return eng.Fori(0, eng.value_load(g.n_pass[0:1, 0:1], min_val=1, max_val=g.PASSES0))

        @block.sync
        def _(sp):
            sp.sem_inc(win_split, 2)
            with passes(sp) as w:
                with sp.Fori(0, RN) as r:
                    sp.wait_ge(tables_made, w + 1)
                    for h in range(2):
                        n = (w * RN + r) * 2 + h
                        first_node = sp.value_load(start_i[0:1, bass.ds(r * 2 + h, 1)], min_val=0,
                                                   max_val=g.N - WIN0)
                        sp.wait_ge(win_split, n + 1)
                        sp.dma_start(win_x[h][:], x[bass.ds(first_node, WIN0), :]).then_inc(win_in[h], 16)

        @block.tensor
        def _(pe):
            def show_ids(n, r, h):
                pe.wait_ge(same_made, n + 1)
                pick = g.ident_bf[0:RN, bass.ds(r, 1)].to_broadcast([RN, P])
                for to, parts in ((dst_b, g.hi_lo[1]), (src_b, g.hi_lo[0])):
                    for c in range(2):
                        cols = slice((2 * h + c) * 512, (2 * h + c + 1) * 512)
                        for k in range(2):
                            last = nc.tensor.matmul(to[:, c * 512:(c + 1) * 512], pick, parts[k][0:RN, cols],
                                                    start=(k == 0), stop=(k == 1))
                last.then_inc(ids_shown, 1)

            pe.sem_inc(same_made, 1)
            pe.sem_inc(msgs_made, 2)
            pe.sem_inc(sums_out, 2)
            pe.wait_ge(msg_init, 1)
            show_ids(0, 0, 0)
            with passes(pe) as w:
                with pe.Fori(0, RN) as r:
                    for h in range(2):
                        n = (w * RN + r) * 2 + h
                        pe.wait_ge(onehot_made, n + 1)
                        for q in range(2):
                            pe.wait_ge(msgs_made, n * 2 + q + 1)
                            for t in range(4 * q, 4 * q + 4):
                                for k in range(3):
                                    last = nc.tensor.matmul(got[:, q, (t % 4) * P:(t % 4 + 1) * P],
                                                            onehot[h][:, t * P:(t + 1) * P], win_s[h][:, k, :],
                                                            start=(k == 0), stop=(k == 2))
                            last.then_inc(fetched, 1)
                        show_ids(n + 1, r + h, 1 - h)
                        for j in range(4):
                            pe.wait_ge(msgs_made, n * 2 + j // 2 + 3)
                            pe.wait_ge(sums_out, n * 4 + j + 1)
                            for i in range(2):
                                t = 2 * j + i
                                last = nc.tensor.matmul(added[:, j % 2, i * R_COLS:(i + 1) * R_COLS],
                                                        same[h][:, t, :], msg[h][:, t, :], start=True, stop=True)
                            last.then_inc(summed, 1)

        @block.scalar
        def _(act):
            with passes(act) as w:
                with act.Fori(0, RN) as r:
                    for h in range(2):
                        n = (w * RN + r) * 2 + h
                        for q in range(2):
                            act.wait_ge(fetched, n * 2 + q + 1)
                            for t in range(4 * q, 4 * q + 4):
                                last = nc.scalar.activation(msg[h][:, t, 0:D], got[:, q, (t % 4) * P:(t % 4 + 1) * P],
                                                            ACT.Copy,
                                                            scale=g.w_col[:, bass.ds(r * ROW_TILES + (h * H + t), 1)])
                            last.then_inc(msgs_made, 1)
                        for j in range(4):
                            act.wait_ge(summed, n * 4 + j + 1)
                            act.wait_ge(turns, n * H + 2 * j + 2)
                            nc.scalar.copy(sums[:, h * H + 2 * j:h * H + 2 * j + 2, :],
                                           added[:, j % 2, 0:2 * R_COLS].rearrange("p (t c) -> p t c", t=2)
                                           ).then_inc(sums_out, 1)

        @block.vector
        def _(dve):
            for h in range(2):
                last = nc.vector.tensor_copy(msg[h][:, :, D:R_COLS],
                                             g.cst[:, C_DUPW:C_DUPW + 2].unsqueeze(1).to_broadcast([P, H, 2]))
            last.then_inc(msg_init, 1)
            halves = g.half_start[:].rearrange("p r h -> p (r h)")
            pid = g.cst[:, C_PID:C_PID + 1]
            spare = g.cst[:, C_SPARE:C_SPARE + 1]
            nc.vector.memset(moved[:, 0:1], 0.0).then_inc(dve_step, 1)
            nc.vector.tensor_copy(moved[:, 1:2], pid).then_inc(dve_step, 1)

            def half(u, r, h):
                n = u * 2 + h
                own = bass.ds(r * 2 + h, 1)
                cols = bass.ds(r * ROW_TILES + h * H, H)
                dve.wait_ge(win_in[h], u * 16 + 16)
                dve.wait_ge(ids_shown, n + 1)
                nc.vector.tensor_copy(win_s[h][:, 0, :], win_x[h][:]).then_inc(part_made, 1)
                dve.wait_ge(part_made, n * 3 + 1)
                nc.vector.tensor_tensor(win_r[h][:], win_x[h][:], win_s[h][:, 0, :],
                                        ALU.subtract).then_inc(win_split, 1)
                dve.wait_ge(win_split, n + 3)
                nc.vector.tensor_copy(win_s[h][:, 1, :], win_r[h][:]).then_inc(part_made, 1)
                dve.wait_ge(part_made, n * 3 + 2)
                nc.vector.tensor_tensor(win_s[h][:, 2, :], win_r[h][:], win_s[h][:, 1, :],
                                        ALU.subtract).then_inc(part_made, 1)
                nc.vector.tensor_scalar(onehot[h][:], dst_b[:], node_id[:, own], None,
                                        ALU.is_equal).then_inc(onehot_made, 1)
                nc.vector.tensor_tensor(same[h][:], src_b[:].rearrange("p (t e) -> p t e", t=H),
                                        g.src_col[:, cols].unsqueeze(2).to_broadcast([P, H, P]),
                                        ALU.is_equal).then_inc(same_made, 1)

            def rows_of(u, r, h):
                n = u * 2 + h
                cols = bass.ds(r * ROW_TILES + h * H, H)
                own = slice(h * H, (h + 1) * H)
                dve.wait_ge(sums_out, n * 4 + 6)
                dve.wait_ge(rows_known, n + 1)
                nc.vector.tensor_scalar(away[:], g.src_col[:, cols], spare, None, ALU.subtract).then_inc(row_step, 1)
                nc.vector.tensor_tensor(first2[:], sums[:, own, D:R_COLS],
                                        g.cst[:, C_DUPT:C_DUPT + 2].unsqueeze(1).to_broadcast([P, H, 2]),
                                        ALU.is_lt).then_inc(row_step, 1)
                dve.wait_ge(row_step, n * 4 + 2)
                nc.vector.tensor_tensor(first[:], first2[:, :, 0], first2[:, :, 1], ALU.mult).then_inc(row_step, 1)
                dve.wait_ge(row_step, n * 4 + 3)
                nc.vector.tensor_tensor(away[:], away[:], first[:], ALU.mult).then_inc(row_step, 1)
                dve.wait_ge(row_step, n * 4 + 4)
                dve.wait_ge(turns, n * H + H)
                nc.vector.tensor_scalar(row_no[:, own], away[:], spare, None, ALU.add).then_inc(rows_known, 1)

            dve.sem_inc(rows_known, 1)
            with passes(dve) as w:
                dve.wait_ge(dve_step, w * 4 + 2)
                nc.vector.tensor_scalar(node_id[:], halves, g.keep[:, 0:1], moved[:, 1:2], ALU.mult,
                                        ALU.add).then_inc(dve_step, 1)
                nc.vector.tensor_scalar(start_i[:], halves, g.keep[:, 0:1], moved[:, 0:1], ALU.mult,
                                        ALU.add).then_inc(tables_made, 1)
                dve.wait_ge(tables_made, w + 1)
                dve.wait_ge(dve_step, w * 4 + 3)
                nc.vector.tensor_scalar(moved[:], moved[:], g.jump[:, 0:1], None, ALU.add).then_inc(dve_step, 1)
                half(w * RN, 0, 0)
                half(w * RN, 0, 1)
                rows_of(w * RN, 0, 0)
                with dve.Fori(1, RN) as r:
                    half(w * RN + r, r, 0)
                    rows_of(w * RN + r - 1, r - 1, 1)
                    half(w * RN + r, r, 1)
                    rows_of(w * RN + r, r, 0)
                rows_of(w * RN + RN - 1, RN - 1, 1)
                dve.sem_inc(dve_step, 2)

        @block.gpsimd
        def _(pool):
            pool.sem_inc(turns, 2 * H - TABLES)
            for k in range(TABLES):
                pool.dma_start(tables[k][g.N:g.N + P, :], g.acc[:, 0:D]).then_inc(table_add[k], 16)
            with passes(pool) as w:
                with pool.Fori(0, RN) as r:
                    for h in range(2):
                        n = (w * RN + r) * 2 + h
                        for t in range(H):
                            k = t % TABLES
                            use = n * (H // TABLES) + t // TABLES
                            if t == 0:
                                pool.wait_ge(rows_known, n + 2)
                            pool.wait_ge(table_add[k], use * 16 + 16)
                            pool.sem_inc(turns, 1)
                            pool.indirect_dma_start(
                                tables[k], bass.IndirectOffsetOnAxis(ap=row_no[:, h * H + t:h * H + t + 1], axis=0),
                                sums[:, h * H + t, 0:D], None, compute_op=ALU.add).then_inc(table_add[k], 16)
            passes_run = pool.value_load(g.n_pass[0:1, 0:1], min_val=1, max_val=g.PASSES0)
            for k in range(TABLES):
                pool.wait_ge(table_add[k], passes_run * (16 * RN * ROW_TILES // TABLES) + 16)
            pool.sem_inc(turns, 1)


BATCH = 4


def norm_stage(nc, g, name, x_in, x_out, tables):
    NB = g.N // (BATCH * P)
    with ExitStack() as ctx:
        def sb(n, shape, dt):
            return ctx.enter_context(nc.sbuf_tensor(f"{name}_{n}", shape, dt))

        def sem(n):
            return ctx.enter_context(nc.semaphore(f"{name}_{n}"))

        n_in = 1 + (len(tables) if tables else 0)
        x_t = [sb(f"x{i}", [P, BATCH, D], F32) for i in range(2)]
        tab_t = [[sb(f"t{i}_{k}", [P, BATCH, D], F32) for k in range(n_in - 1)] for i in range(2)]
        feat = [sb(f"feat{i}", [P, BATCH, P], F32) for i in range(2)]
        z = [sb(f"z{i}", [P, BATCH, D], F32) for i in range(2)]
        stats = sb("stats", [P, BATCH, 6], F32)
        mv = sb("mv", [P, BATCH, 2], F32)
        var = sb("var", [P, BATCH], F32)
        std = sb("std", [P, BATCH], F32)
        rstd = sb("rstd", [P, BATCH], F32)
        pre = ctx.enter_context(nc.psum_tensor(f"{name}_pre", [P, 2, 512], F32))
        y = ctx.enter_context(nc.psum_tensor(f"{name}_y", [P, 2, 512], F32))

        loaded = [sem(f"loaded{i}") for i in range(2)]
        free = sem("free")
        pre_made = sem("pre_made")
        feat_made = sem("feat_made")
        y_made = sem("y_made")
        step = sem("step")
        aggr_turn = sem("aggr_turn")
        var_made = sem("var_made")
        std_made = sem("std_made")
        normed = sem("normed")
        stored = [sem(f"stored{i}") for i in range(2)]
        block = ctx.enter_context(nc.Block())

        def tiles(ap):
            return ap.rearrange("(b p a) d -> b p a d", p=P, a=BATCH)

        @block.sync
        def _(sp):
            sp.sem_inc(free, 2)
            with sp.Fori(0, NB // 2) as i:
                for s in range(2):
                    b = i * 2 + s
                    sp.wait_ge(free, b + 1)
                    for k in range(n_in - 1):
                        sp.dma_start(tab_t[s][k][:], tiles(tables[k][0:g.N, :])[bass.ds(b, 1)].squeeze(0)
                                     ).then_inc(loaded[s], 16)
                    sp.dma_start(x_t[s][:], tiles(x_in)[bass.ds(b, 1)].squeeze(0)).then_inc(loaded[s], 16)

        @block.tensor
        def _(pe):
            ident = g.cst[:, C_IDENT:C_IDENT + P]
            if tables:
                pe.sem_inc(feat_made, 2)
            with pe.Fori(0, NB // 2) as i:
                for s in range(2):
                    b = i * 2 + s
                    if tables:
                        pe.wait_ge(loaded[s], i * (16 * n_in) + 16 * n_in)
                        pe.wait_ge(feat_made, b + 1)
                        for a in range(BATCH):
                            for k in range(len(tables)):
                                last = nc.tensor.matmul(pre[:, s, a * P:(a + 1) * P], tab_t[s][k][:, a, :], ident,
                                                        start=(k == 0), stop=(k == len(tables) - 1))
                        last.then_inc(pre_made, 1)
                        pe.wait_ge(feat_made, b + 3)
                        for a in range(BATCH):
                            last = nc.tensor.matmul(y[:, s, a * P:(a + 1) * P], feat[s][:, a, :], g.w_t[:],
                                                    start=True, stop=True)
                        last.then_inc(y_made, 1)
                    else:
                        pe.wait_ge(feat_made, b + 1)
                        pe.wait_ge(free, b + 1)
                        for a in range(BATCH):
                            last = nc.tensor.transpose(y[:, s, a * P:(a + 1) * P], feat[s][:, a, :], ident)
                        last.then_inc(y_made, 1)

        @block.scalar
        def _(act):
            if not tables:
                act.sem_inc(y_made, 2)

            def store(b, s):
                act.wait_ge(var_made, b + 1)
                nc.scalar.activation(std[:], var[:], ACT.Sqrt).then_inc(std_made, 1)
                act.wait_ge(normed, b + 1)
                act.dma_start(tiles(x_out)[bass.ds(b, 1)].squeeze(0), z[s][:]).then_inc(stored[s], 16)

            def features(b, s):
                if tables:
                    act.wait_ge(pre_made, b + 1)
                    nc.scalar.copy(feat[s][:].rearrange("p a n -> p (a n)"), pre[:, s, :]).then_inc(feat_made, 1)
                else:
                    act.wait_ge(y_made, b + 1)
                    nc.scalar.copy(feat[s][:], g.acc[:, bass.ds(b * (BATCH * P), BATCH * P)].rearrange(
                        "f (p a) -> f a p", a=BATCH)).then_inc(feat_made, 1)

            features(0, 0)
            features(1, 1)
            store(0, 0)
            with act.Fori(1, NB // 2) as i:
                features(i * 2, 0)
                store(i * 2 - 1, 1)
                features(i * 2 + 1, 1)
                store(i * 2, 0)
            store(NB - 1, 1)
            for s in range(2):
                act.wait_ge(stored[s], 16 * (NB // 2))

        @block.vector
        def _(dve):
            y_credit = 0 if tables else 2

            def norm(i, s, first):
                b = i * 2 + s
                dve.wait_ge(y_made, b + 1 + y_credit)
                dve.wait_ge(loaded[s], i * (16 * n_in) + 16 * n_in)
                if not first:
                    dve.wait_ge(stored[s], i * 16)
                nc.vector.tensor_tensor(z[s][:], x_t[s][:], y[:, s, :].rearrange("p (a d) -> p a d", a=BATCH),
                                        ALU.add).then_inc(free, 1)
                dve.wait_ge(free, b + 3)
                for a in range(BATCH):
                    nc.vector.bn_stats(stats[:, a, :], z[s][:, a, :]).then_inc(step, 1)
                dve.wait_ge(step, b * 9 + 4)
                dve.sem_inc(aggr_turn, 1)
                for a in range(BATCH):
                    nc.vector.bn_aggr(mv[:, a, :], stats[:, a, :]).then_inc(step, 1)
                dve.wait_ge(step, b * 9 + 8)
                nc.vector.tensor_scalar(var[:], mv[:, :, 1], EPS, None, ALU.add).then_inc(var_made, 1)
                dve.wait_ge(std_made, b + 1)
                nc.vector.reciprocal(rstd[:], std[:]).then_inc(step, 1)
                dve.wait_ge(step, b * 9 + 9)
                for a in range(BATCH):
                    last = nc.vector.tensor_scalar(z[s][:, a, :], z[s][:, a, :], mv[:, a, 0:1], rstd[:, a:a + 1],
                                                   ALU.subtract, ALU.mult)
                last.then_inc(normed, 1)
                dve.wait_ge(normed, b + 1)

            norm(0, 0, True)
            norm(0, 1, True)
            with dve.Fori(1, NB // 2) as i:
                norm(i, 0, False)
                norm(i, 1, False)


def layer1(nc, g, x1, w_tp):
    RN, TN = g.RN, g.TN
    H, Q, R = HALF_TILES, QUAD_TILES, ROW_TILES
    with ExitStack() as ctx:
        def sb(name, shape, dt):
            return ctx.enter_context(nc.sbuf_tensor(name, shape, dt))

        def sem(name):
            return ctx.enter_context(nc.semaphore(name))

        w_scalar = sb("w_scalar", [P, MUL], F32)
        w_vec = [sb(f"w_vec{i}", [P, MUL], F32) for i in range(2)]
        mix = sb("mix", [P, NA, D], F32)
        win_start = sb("win_start", [P, TN], F32)
        dst_rel = sb("dst_rel", [P, TN], F32)
        off_f = sb("off_f", [P, TN], F32)
        tile_off = sb("tile_off", [P, TN], I32)
        quad_off = sb("quad_off", [P, TN // Q], I32)
        row_start = sb("row_start", [P, RN], I32)
        moved = sb("l1_moved", [P, 1], F32)
        zero_bf = sb("zero_bf", [P, NA * QUAD_WIN], BF16)
        ids = [sb(f"ids{h}", [P, H], I32) for h in range(2)]
        feat = sb("feat", [P, R, D], F32)
        hot = sb("hot", [P, H, WIN], F32)
        attr_hot = [sb(f"attr_hot{h}", [P, H, NA, WIN], F32) for h in range(2)]
        group = [sb(f"group{z}", [P, NA, GROUP_WIN], F32) for z in range(2)]
        quad = ctx.enter_context(nc.psum_tensor("quad", [P, Q, 512], F32))
        mixed = ctx.enter_context(nc.psum_tensor("mixed", [P, 2, 512], F32))

        weights_in = sem("weights_in")
        setup_step = sem("l1_setup_step")
        tables_made = sem("l1_tables_made")
        ids_made = sem("ids_made")
        feat_in = [sem(f"feat_in{t}") for t in range(R)]
        feat_used = sem("feat_used")
        hot_step = sem("hot_step")
        hot_made = sem("hot_made")
        quad_added = sem("quad_added")
        group_zero = sem("group_zero")
        group_used = sem("group_used")
        acc_added = sem("acc_added")
        pool_turn = sem("pool_turn")
        block = ctx.enter_context(nc.Block())

        def passes(eng):
            return eng.Fori(0, eng.value_load(g.n_pass[0:1, 1:2], min_val=1, max_val=g.PASSES1))

        @block.sync
        def _(sp):
            w0, w1, w2, w3, w4 = [w.rearrange("u v w -> (u v) w") for w in w_tp]
            loads = [(w_scalar, w0, w3), (w_vec[0], w1, w2), (w_vec[1], w1, w4)]
            for to, from_scalars, from_vectors in loads:
                sp.dma_start(to[0:MUL, :], from_scalars).then_inc(weights_in, 16)
                for i in range(3):
                    sp.dma_start(to[MUL + i:P:3, :], from_vectors).then_inc(weights_in, 16)

        @block.gpsimd
        def _(pool):
            with passes(pool) as w:
                with pool.Fori(0, RN) as r:
                    u = w * RN + r
                    for q in range(R // Q):
                        if q % 2 == 0:
                            pool.wait_ge(ids_made, u * 2 + (q // 2 + 1))
                        pool.wait_ge(feat_used, u * R + 4 * q + 4)
                        pool.sem_inc(pool_turn, 1)
                        for t in range(Q * q, Q * q + Q):
                            pool.indirect_dma_start(
                                feat[:, t, :], None, x1,
                                bass.IndirectOffsetOnAxis(ap=ids[t // H][:, t % H:t % H + 1], axis=0),
                            ).then_inc(feat_in[t], 16)
            passes_run = pool.value_load(g.n_pass[0:1, 1:2], min_val=1, max_val=g.PASSES1)
            for t in range(R):
                pool.wait_ge(feat_in[t], passes_run * (16 * RN))
            pool.sem_inc(pool_turn, 1)

        @block.scalar
        def _(act):
            act.sem_inc(group_used, 2)
            for h in range(2):
                nc.scalar.copy(ids[h][:], g.src_col[:, h * H:h * H + H]).then_inc(ids_made, 1)
            with passes(act) as w:
                with act.Fori(0, RN // 2) as i:
                    for z in range(2):
                        r = i * 2 + z
                        u = w * RN + r
                        act.wait_ge(group_used, u + 1)
                        nc.scalar.memzero(group[z][:]).then_inc(group_zero, 1)
                        for h in range(2):
                            for t in range(h * H, h * H + H):
                                act.wait_ge(feat_in[t], u * 16 + 16)
                            nc.scalar.copy(ids[h][:], g.src_col[:, bass.ds(r * R + (R + h * H), H)]
                                           ).then_inc(ids_made, 1)

        @block.tensor
        def _(pe):
            pe.sem_inc(feat_used, R)
            pe.sem_inc(quad_added, R // Q)
            pe.sem_inc(acc_added, 2)
            with passes(pe) as w:
                with pe.Fori(0, RN // 2) as i:
                    pe.wait_ge(tables_made, w + 1)
                    for z in range(2):
                        r = i * 2 + z
                        u = w * RN + r
                        for q in range(R // Q):
                            pe.wait_ge(quad_added, u * 4 + q + 1)
                            nc.tensor.matmul(quad[:, q, 0:NA * QUAD_WIN], zero_bf[0:1, 0:P], zero_bf[0:1, :],
                                             start=True, stop=False, skip_group_check=True)
                            if q % 2 == 0:
                                pe.wait_ge(hot_made, u * 2 + (q // 2 + 2))
                            bank = quad[:, q, 0:NA * QUAD_WIN].rearrange("p (m n) -> p m n", m=NA)
                            for t in range(Q * q, Q * q + Q):
                                if t % Q:
                                    off = pe.value_load(tile_off[0:1, bass.ds(r * R + t, 1)], min_val=0,
                                                        max_val=QUAD_WIN - WIN)
                                else:
                                    off = 0
                                pe.wait_ge(feat_in[t], u * 16 + 16)
                                nc.tensor.matmul(bank[:, :, bass.ds(off, WIN)], feat[:, t, :],
                                                 attr_hot[t // H][:, t % H, :, :], start=False,
                                                 stop=(t % Q == Q - 1), skip_group_check=True
                                                 ).then_inc(feat_used, 1)
                        pe.wait_ge(quad_added, u * 4 + 8)
                        pe.wait_ge(acc_added, u + 1)
                        for m in range(NA):
                            last = nc.tensor.matmul(mixed[:, z, 0:GROUP_WIN], mix[:, m, :], group[z][:, m, :],
                                                    start=(m == 0), stop=(m == NA - 1))
                        last.then_inc(group_used, 1)

        @block.vector
        def _(dve):
            coef = g.cst[:, C_COEF:C_COEF + 4 * NA].rearrange("p (m c) -> p m c", c=4)
            nc.vector.memset(zero_bf[:], 0.0)
            nc.vector.memset(g.acc[:], 0.0)
            nc.vector.memset(moved[:], 0.0).then_inc(setup_step, 1)
            dve.wait_ge(weights_in, 16 * 12)
            nc.vector.tensor_tensor(mix[:, :, 0:MUL], w_scalar[:].unsqueeze(1).to_broadcast([P, NA, MUL]),
                                    coef[:, :, 0:1].to_broadcast([P, NA, MUL]), ALU.mult)
            vec = mix[:, :, MUL:D].rearrange("p m (w k) -> p m w k", k=3)
            for wv, m0, m1 in ((w_vec[0], 0, 4), (w_vec[1], 4, NA)):
                s4 = [P, m1 - m0, MUL, 3]
                nc.vector.tensor_tensor(vec[:, m0:m1], wv[:].unsqueeze(1).unsqueeze(3).to_broadcast(s4),
                                        coef[:, m0:m1, 1:4].unsqueeze(2).to_broadcast(s4), ALU.mult)
            dve.sem_inc(hot_made, 1)

            def hots(u, r, h):
                cols = bass.ds(r * R + h * H, H)
                s3, s4 = [P, H, WIN], [P, H, NA, WIN]
                dve.wait_ge(hot_made, u * 2 + (h + 1))
                nc.vector.tensor_tensor(hot[:], g.cst[:, C_IOTA:C_IOTA + WIN].unsqueeze(1).to_broadcast(s3),
                                        dst_rel[:, cols].unsqueeze(2).to_broadcast(s3),
                                        ALU.is_equal).then_inc(hot_step, 1)
                dve.wait_ge(hot_step, u * 2 + (h + 1))
                dve.wait_ge(feat_used, u * R + (h * H + H))
                nc.vector.tensor_tensor(attr_hot[h][:], hot[:].unsqueeze(2).to_broadcast(s4),
                                        g.attr_col[:, cols, :].unsqueeze(3).to_broadcast(s4),
                                        ALU.mult).then_inc(hot_made, 1)

            def add_quads(u, r, z):
                for q in range(R // Q):
                    if q:
                        off = dve.value_load(quad_off[0:1, bass.ds(r * (R // Q) + q, 1)], min_val=0,
                                             max_val=GROUP_WIN - QUAD_WIN)
                        dve.wait_ge(quad_added, u * 4 + (q + 4))
                    else:
                        off = 0
                        dve.wait_ge(group_zero, u + 1)
                    dve.wait_ge(feat_used, u * R + (R + 4 * q + 4))
                    to = group[z][:, :, bass.ds(off, QUAD_WIN)]
                    nc.vector.tensor_tensor(to, to, quad[:, q, 0:NA * QUAD_WIN].rearrange("p (m n) -> p m n", m=NA),
                                            ALU.add).then_inc(quad_added, 1)

            def add_row(u, r, z):
                at = dve.value_load(row_start[0:1, bass.ds(r, 1)], min_val=0, max_val=g.N - 1)
                dve.wait_ge(group_used, u + 3)
                dve.wait_ge(acc_added, u + 2)
                to = g.acc[:, bass.ds(at, GROUP_WIN)]
                nc.vector.tensor_tensor(to, to, mixed[:, z, 0:GROUP_WIN], ALU.add).then_inc(acc_added, 1)

            with passes(dve) as w:
                S = 8
                n = w * S
                keep = g.keep[:, 1:2]
                starts = g.tile_start[:]
                by4 = starts.rearrange("p (a b) -> p a b", b=Q)
                off4 = off_f[:].rearrange("p (a b) -> p a b", b=Q)
                quad_first = starts.rearrange("p (a b c) -> p a b c", b=R // Q, c=Q)[:, :, :, 0]
                offq = off_f[:, 0:TN // Q].rearrange("p (a b) -> p a b", b=R // Q)
                dve.wait_ge(setup_step, n + 1)
                nc.vector.tensor_scalar(win_start[:], starts, keep, moved[:], ALU.mult, ALU.add).then_inc(setup_step, 1)
                nc.vector.tensor_tensor(off4, by4, by4[:, :, 0:1].to_broadcast([P, TN // Q, Q]),
                                        ALU.subtract).then_inc(setup_step, 1)
                dve.wait_ge(setup_step, n + 3)
                nc.vector.tensor_tensor(dst_rel[:], g.dst_col[:], win_start[:], ALU.subtract).then_inc(setup_step, 1)
                nc.vector.tensor_scalar(tile_off[:], off_f[:], keep, None, ALU.mult).then_inc(setup_step, 1)
                nc.vector.tensor_copy(row_start[:], win_start[:].rearrange("p (a b) -> p a b", b=R)[:, :, 0]
                                      ).then_inc(setup_step, 1)
                dve.wait_ge(setup_step, n + 6)
                nc.vector.tensor_tensor(offq, quad_first, quad_first[:, :, 0:1].to_broadcast([P, RN, R // Q]),
                                        ALU.subtract).then_inc(setup_step, 1)
                nc.vector.tensor_tensor(moved[:], moved[:], g.jump[:, 1:2], ALU.add).then_inc(setup_step, 1)
                dve.wait_ge(setup_step, n + 8)
                nc.vector.tensor_scalar(quad_off[:], off_f[:, 0:TN // Q], keep, None, ALU.mult).then_inc(setup_step, 1)
                dve.wait_ge(setup_step, n + 9)
                dve.sem_inc(tables_made, 1)

                def row_pair(i, first):
                    for z in range(2):
                        r = i * 2 + z
                        u = w * RN + r
                        hots(u, r, 0)
                        if z or not first:
                            add_row(u - 1, r - 1, 1 - z)
                        hots(u, r, 1)
                        add_quads(u, r, z)

                row_pair(0, True)
                with dve.Fori(1, RN // 2) as i:
                    row_pair(i, False)
                add_row(w * RN + RN - 1, RN - 1, 1)


_INS = ["x", "src", "dst", "edge_attr_9", "edge_weight", "L0_gnn_W"] + [f"L1_gnn_w{k}" for k in range(5)]


def kernel(**inputs):
    import concourse.bacc as _bacc
    from concourse.bass_utils import run_bass_kernel_spmd as _run

    nc = _bacc.Bacc("TRN2", target_bir_lowering=False, num_devices=1)
    arrays, args = {}, []
    for name in _INS + ["constants"]:
        a = np.ascontiguousarray(inputs[name] if name in inputs else constants(inputs["x"].shape[0]))
        arrays[f"in_{name}"] = a
        args.append(nc.dram_tensor(f"in_{name}", a.shape, mybir.dt.from_np(a.dtype), kind="ExternalInput").ap())
    n = inputs["x"].shape[0]
    out = nc.dram_tensor("out_0", (n, D), F32, kind="ExternalOutput").ap()
    tables = [nc.dram_tensor(f"table{k}", (n + P, D), F32, kind="Internal").ap() for k in range(TABLES)]
    x1 = nc.dram_tensor("x1", (n, D), F32, kind="Internal").ap()
    x, src, dst, attr, weight, w_lin, *w_tp, consts = args
    gnn_kernel(nc, x, src, dst, attr, weight, w_lin, w_tp, consts, out, tables, x1)
    return _run(nc, [arrays], core_ids=[0]).results[0]["out_0"]
```

```python
from contextlib import ExitStack

import numpy as np

import concourse.bass as bass
from concourse import mybir

ALU = mybir.AluOpType
ACT = mybir.ActivationFunctionType
AX_X = mybir.AxisListType.X
F32 = mybir.dt.float32
BF16 = mybir.dt.bfloat16
I32 = mybir.dt.int32

P = 128
D = 128
MUL = 32
NA = 9
ROW_TILES = 16
HALF_TILES = 8
QUAD_TILES = 4
ROW_EDGES = ROW_TILES * P
TABLES = 4
ZERO_CUTS = 4
EPS = 1e-5
NEIGHBORS = 10.0

WIN0 = 128
WIN = 16
QUAD_WIN = 56
GROUP_WIN = 192
TILE_BITS = 6
QUAD_BITS = 8

C_IDENT = 0
C_COEF = C_IDENT + P
C_DUPW = C_COEF + 4 * NA
C_DUPT = C_DUPW + 2
C_IOTA = C_DUPT + 2
C_PID = C_IOTA + WIN
C_SPARE = C_PID + 1
C_ALL = C_SPARE + 1


def wigner_121():
    c = np.zeros((3, 5, 3))
    c[0, 0, 2] = c[2, 0, 0] = 1.0
    c[0, 1, 1] = c[1, 1, 0] = 1.0
    c[0, 2, 0] = c[2, 2, 2] = -1.0 / np.sqrt(3.0)
    c[1, 2, 1] = 2.0 / np.sqrt(3.0)
    c[1, 3, 2] = c[2, 3, 1] = 1.0
    c[0, 4, 0] = -1.0
    c[2, 4, 2] = 1.0
    return c / np.sqrt(10.0)


def constants(n_nodes):
    c = np.zeros((P, C_ALL), np.float64)
    p = np.arange(P)
    c[:, C_IDENT:C_IDENT + P] = np.eye(P)
    coef = np.zeros((P, NA, 4))
    to_scalar = np.sqrt(1.0 / (2 * MUL)) / np.sqrt(NEIGHBORS)
    to_vector = np.sqrt(3.0 / (3 * MUL)) / np.sqrt(NEIGHBORS)
    dot = 1.0 / np.sqrt(3.0)
    i = np.arange(P - MUL) % 3
    coef[:MUL, 0, 0] = to_scalar
    coef[MUL:, 0, 1:] = np.eye(3)[i] * dot * to_vector
    for j in range(3):
        coef[:MUL, 1 + j, 1 + j] = dot * to_vector
        coef[MUL:, 1 + j, 0] = (i == j) * dot * to_scalar
    for j in range(5):
        coef[MUL:, 4 + j, 1:] = wigner_121()[i, j] * to_vector
    c[:, C_COEF:C_COEF + 4 * NA] = coef.reshape(P, -1)
    half = P // 2
    w = 2.0 ** (126 - 2 * (p % half))
    c[:half, C_DUPW] = w[:half]
    c[half:, C_DUPW + 1] = w[half:]
    c[:half, C_DUPT] = 2 * w[:half]
    c[:half, C_DUPT + 1] = 3e38
    c[half:, C_DUPT] = 0.5
    c[half:, C_DUPT + 1] = 2 * w[half:]
    c[:, C_IOTA:C_IOTA + WIN] = np.arange(WIN)
    c[:, C_PID] = p
    c[:, C_SPARE] = n_nodes + p
    return c.astype(np.float32)


class Shared:
    pass


def gnn_kernel(nc, x, src, dst, attr, weight, w_lin, w_tp, consts, out, tables, x1):
    g = Shared()
    g.N = x.shape[0]
    g.E = src.shape[0]
    g.RN = g.E // ROW_EDGES
    g.TN = g.E // P
    g.PASSES0 = g.N // WIN0
    g.PASSES1 = g.N // WIN
    assert g.E % (2 * ROW_EDGES) == 0 and g.RN <= P and g.N % 1024 == 0
    with ExitStack() as ctx:
        def sb(name, shape, dt):
            return ctx.enter_context(nc.sbuf_tensor(name, shape, dt))

        g.cst = sb("cst", [P, C_ALL], F32)
        g.ident_bf = sb("ident_bf", [P, g.RN + 1], BF16)
        g.acc = sb("acc", [P, g.N + GROUP_WIN], F32)
        g.src_col = sb("src_col", [P, g.TN + ROW_TILES], F32)
        g.dst_col = sb("dst_col", [P, g.TN], F32)
        g.tile_start = sb("tile_start", [P, g.TN], F32)
        g.keep = sb("keep", [P, 2], F32)
        g.jump = sb("jump", [P, 2], F32)
        g.n_pass = sb("n_pass", [P, 2], I32)
        g.w_t = sb("w_t", [P, D], F32)
        g.mix = sb("mix", [P, NA, D], F32)
        g.dst_rel = sb("dst_rel", [P, g.TN], F32)
        g.tile_offs = sb("tile_offs", [P, g.TN // QUAD_TILES], I32)
        g.quad_offs = sb("quad_offs", [P, g.RN], I32)
        g.row_f = sb("row_f", [P, g.RN], F32)
        g.row_start = sb("row_start", [P, g.RN], I32)
        g.table_add = [ctx.enter_context(nc.semaphore(f"table_add{k}")) for k in range(TABLES)]
        with ExitStack() as mid:
            def sm(name, shape, dt):
                return mid.enter_context(nc.sbuf_tensor(name, shape, dt))
            g.w_col = sm("w_col", [P, g.TN], F32)
            g.half_start = sm("half_start", [P, g.RN, 2], F32)
            g.hi_lo = [[sm(f"{n}_{h}", [P, ROW_EDGES], BF16) for h in ("hi", "lo")] for n in ("src", "dst")]
            setup(nc, g, src, dst, weight, w_lin, consts, tables)
            layer0(nc, g, x, tables, w_tp)
        norm_stage(nc, g, "norm0", x, x1, tables)
        layer1(nc, g, x1, attr)
        norm_stage(nc, g, "norm1", x1, out, None)


def link_farthest(nc, link, a, b, far, reach, miss, limit):
    link(nc.vector.scalar_tensor_tensor(out=far, in0=a, scalar=-limit / 2.0, in1=b, op0=ALU.add, op1=ALU.subtract))
    link(nc.vector.tensor_reduce(reach, far.rearrange("p a b -> p (a b)"), AX_X, ALU.max, apply_absolute_value=True))
    link(nc.vector.tensor_scalar(miss, reach, limit / 2.0, None, ALU.is_gt))


def fill(pool, g, tables, k):
    n_zero = (g.N + P) // ZERO_CUTS
    pool.dma_start(tables[k].rearrange("n d -> (n d)").rearrange("(p c f) -> p c f", p=P, c=ZERO_CUTS),
                   g.acc[:, 0:n_zero].unsqueeze(1).to_broadcast([P, ZERO_CUTS, n_zero])
                   ).then_inc(g.table_add[k], 16)


def setup(nc, g, src, dst, weight, w_lin, consts, tables):
    RN, TN = g.RN, g.TN
    with ExitStack() as ctx:
        def sb(name, shape, dt):
            return ctx.enter_context(nc.sbuf_tensor(name, shape, dt))

        def sem(name):
            return ctx.enter_context(nc.semaphore(name))

        rows_i = [sb(f"rows_i{i}", [P, ROW_EDGES], I32) for i in range(2)]
        rows_f = [sb(f"rows_f{i}", [P, ROW_EDGES], F32) for i in range(3)]
        w_in = sb("w_in", [P, D], F32)
        ones = sb("ones", [P, P], F32)
        far = sb("far", [P, TN], F32)
        reach = sb("reach", [P, 1], F32)
        miss = sb("miss", [P, 4], F32)
        some = sb("some", [P, 4], F32)
        some1 = sb("some1", [P, 1], F32)
        pt = ctx.enter_context(nc.psum_tensor("pt", [P, 4, 512], F32))
        pa = ctx.enter_context(nc.psum_tensor("pa", [P, 2, 512], F32))

        consts_in = sem("consts_in")
        rows_in = [sem(f"rows_in{i}") for i in range(3)]
        zeroed = sem("zeroed")
        rows_made = sem("rows_made")
        ident_made = sem("ident_made")
        split_made = sem("split_made")
        group_done = sem("group_done")
        group_out = sem("group_out")
        miss_made = sem("miss_made")
        miss_sum = sem("miss_sum")
        dve_step = sem("dve_step")
        wt_done = sem("wt_done")

        col_groups = [(which, q) for q in range(4) for which in range(3)]
        n_groups = len(col_groups) + 4
        n_zero = (g.N + P) // ZERO_CUTS
        block = ctx.enter_context(nc.Block(no_gpsimd_drain=True))

        @block.sync
        def _(sp):
            sp.dma_start(g.cst[:], consts).then_inc(consts_in, 16)
            sp.dma_start(w_in[:], w_lin).then_inc(consts_in, 16)
            sp.dma_start(rows_i[0][0:RN, :], src.rearrange("(r c) -> r c", r=RN)).then_inc(rows_in[0], 16)
            sp.dma_start(rows_i[1][0:RN, :], dst.rearrange("(r c) -> r c", r=RN)).then_inc(rows_in[1], 16)
            sp.dma_start(rows_f[2][0:RN, :], weight.rearrange("(r c) -> r c", r=RN)).then_inc(rows_in[2], 16)

        @block.gpsimd
        def _(pool):
            pool.wait_ge(zeroed, 1)
            for k in range(TABLES - 1):
                fill(pool, g, tables, k)

        @block.vector
        def _(dve):
            steps = [0]

            def link(ins):
                steps[0] += 1
                ins.then_inc(dve_step, 1)
                dve.wait_ge(dve_step, steps[0])

            nc.vector.memset(g.acc[:, 0:n_zero], 0.0).then_inc(zeroed, 1)
            dve.wait_ge(consts_in, 32)
            nc.vector.tensor_copy(g.ident_bf[:, 0:RN], g.cst[:, C_IDENT:C_IDENT + RN])
            nc.vector.tensor_copy(g.ident_bf[:, RN:RN + 1], g.cst[:, C_IDENT:C_IDENT + 1]).then_inc(ident_made, 1)
            for i in range(2):
                dve.wait_ge(rows_in[i], 16)
                nc.vector.tensor_copy(rows_f[i][0:RN, :], rows_i[i][0:RN, :]).then_inc(rows_made, 1)
            dve.wait_ge(rows_made, 2)
            for i in (1, 0):
                hi, lo = g.hi_lo[i]
                link(nc.vector.tensor_scalar(rows_i[i][0:RN, :], rows_i[i][0:RN, :], P - 1, None, ALU.bitwise_and))
                link(nc.vector.tensor_copy(lo[0:RN, :], rows_i[i][0:RN, :]))
                nc.vector.tensor_tensor(hi[0:RN, :], rows_f[i][0:RN, :], rows_i[i][0:RN, :],
                                        ALU.subtract).then_inc(split_made, 1)
            nc.vector.memset(g.acc[:, n_zero:], 0.0)
            nc.vector.memset(ones[:], 1.0)
            link(nc.vector.memset(miss[:], 0.0))
            first = rows_f[1][0:RN, :].rearrange("r (a b e) -> r a b e", b=QUAD_TILES, e=P)[:, :, :, 0]
            n_quads = ROW_TILES // QUAD_TILES
            tests = [(first, first[:, :, 0:1], QUAD_TILES, QUAD_WIN - WIN),
                     (first[:, :, 0:1], first[:, 0:1, 0:1], 1, GROUP_WIN - QUAD_WIN)]
            for k, (a, b, n, limit) in enumerate(tests):
                link_farthest(nc, link, a, b.to_broadcast([RN, n_quads, n]),
                              far[0:RN, 0:n_quads * n].rearrange("p (a b) -> p a b", b=n), reach[0:RN, :],
                              miss[0:RN, 2 + k:3 + k], float(limit))
            dve.wait_ge(group_out, n_groups)
            nc.vector.tensor_copy(g.src_col[:, TN:TN + ROW_TILES], g.src_col[:, 0:ROW_TILES])
            starts = g.tile_start[:].rearrange("p (s t) -> p s t", t=HALF_TILES)
            halves = g.half_start[:].rearrange("p r h -> p (r h)")
            link(nc.vector.tensor_scalar(halves, starts[:, :, 0], float(g.N - WIN0), None, ALU.min))
            by8 = [t.rearrange("p (a b) -> p a b", b=HALF_TILES) for t in (g.dst_col[:], g.tile_start[:], far[:])]
            link_farthest(nc, link, by8[0], halves.unsqueeze(2).to_broadcast([P, TN // HALF_TILES, HALF_TILES]),
                          by8[2], reach[:], miss[:, 0:1], WIN0 - 1.0)
            link_farthest(nc, link, *by8, reach[:], miss[:, 1:2], WIN - 1.0)
            dve.sem_inc(miss_made, 1)
            dve.wait_ge(miss_sum, 1)
            link(nc.vector.tensor_scalar(some[:], pa[:, 0, 0:4], 0.5, None, ALU.is_gt))
            link(nc.vector.tensor_reduce(some1[:], some[:, 1:4], AX_X, ALU.max))
            for l, (win, passes, on) in enumerate(((WIN0, g.PASSES0, some[:, 0:1]), (WIN, g.PASSES1, some1[:]))):
                nc.vector.tensor_scalar(g.keep[:, l:l + 1], on, -1.0, 1.0, ALU.mult, ALU.add)
                nc.vector.tensor_scalar(g.jump[:, l:l + 1], on, float(win), None, ALU.mult)
                nc.vector.tensor_scalar(g.n_pass[:, l:l + 1], on, float(passes - 1), 1.0, ALU.mult, ALU.add)

        @block.tensor
        def _(pe):
            ident = g.cst[:, C_IDENT:C_IDENT + P]
            ident_rows = g.cst[0:RN, C_IDENT:C_IDENT + RN]
            pe.wait_ge(consts_in, 32)
            n = 0
            for which, q in col_groups:
                if which < 2:
                    pe.wait_ge(rows_made, which + 1)
                else:
                    pe.wait_ge(rows_in[2], 16)
                if n >= 4:
                    pe.wait_ge(group_out, n - 3)
                for j in range(4):
                    k = 4 * q + j
                    last = nc.tensor.transpose(pt[:, n % 4, j * P:j * P + RN],
                                               rows_f[which][0:RN, k * P:(k + 1) * P], ident_rows)
                last.then_inc(group_done, 1)
                n += 1
            pe.wait_ge(ident_made, 1)
            pe.wait_ge(split_made, 1)
            for q in range(4):
                pe.wait_ge(group_out, n - 3)
                for j in range(4):
                    k = 4 * q + j
                    for part in range(2):
                        first = g.hi_lo[1][part][0:RN, k * P:k * P + 1].to_broadcast([RN, P])
                        last = nc.tensor.matmul(pt[:, n % 4, j * P:j * P + RN], first, g.ident_bf[0:RN, 0:RN],
                                                start=(part == 0), stop=(part == 1))
                last.then_inc(group_done, 1)
                n += 1
            nc.tensor.transpose(pa[:, 1, 0:P], w_in[:], ident).then_inc(wt_done, 1)
            pe.wait_ge(miss_made, 1)
            nc.tensor.matmul(pa[:, 0, 0:4], ones[:], miss[:], start=True, stop=True).then_inc(miss_sum, 1)

        @block.scalar
        def _(act):
            cols = [g.src_col, g.dst_col, g.w_col]
            for n in range(n_groups):
                if n < len(col_groups):
                    which, q = col_groups[n]
                    dest = cols[which]
                else:
                    q, dest = n - len(col_groups), g.tile_start
                act.wait_ge(group_done, n + 1)
                o = dest[:, 0:TN].rearrange("p (r k) -> p k r", k=ROW_TILES)[:, 4 * q:4 * q + 4, :]
                i = pt[:, n % 4, :].rearrange("p (j r) -> p j r", j=4)[:, :, 0:RN]
                nc.scalar.copy(o, i).then_inc(group_out, 1)
            act.wait_ge(wt_done, 1)
            nc.scalar.copy(g.w_t[:], pa[:, 1, 0:P])


def layer0(nc, g, x, tables, w_tp):
    RN = g.RN
    H = HALF_TILES
    R_COLS = D + 2
    with ExitStack() as ctx:
        def sb(name, shape, dt):
            return ctx.enter_context(nc.sbuf_tensor(name, shape, dt))

        def sem(name):
            return ctx.enter_context(nc.semaphore(name))

        node_id = sb("node_id", [P, RN * 2], F32)
        start_i = sb("start_i", [P, RN * 2], I32)
        moved = sb("moved", [P, 2], F32)
        win_x = [sb(f"win_x{i}", [P, D], F32) for i in range(2)]
        win_r = [sb(f"win_r{i}", [P, D], F32) for i in range(2)]
        win_s = [sb(f"win_s{i}", [P, 3, D], BF16) for i in range(2)]
        onehot = [sb(f"onehot{i}", [P, H * P], BF16) for i in range(2)]
        same = [sb(f"same{i}", [P, H, P], F32) for i in range(2)]
        msg = [sb(f"msg{i}", [P, H, R_COLS], F32) for i in range(2)]
        sums = sb("sums", [P, 2 * H, R_COLS], F32)
        row_no = sb("row_no", [P, 2 * H], I32)
        first2 = sb("first2", [P, H, 2], F32)
        first = sb("first", [P, H], F32)
        away = sb("away", [P, H], F32)
        w_scalar = sb("w_scalar", [P, MUL], F32)
        w_vec = [sb(f"w_vec{i}", [P, MUL], F32) for i in range(2)]
        off_f = sb("off_f", [P, g.TN], F32)
        word_f = sb("word_f", [P, g.TN // QUAD_TILES], F32)
        dst_b = ctx.enter_context(nc.psum_tensor("dst_b", [P, H * P], F32))
        src_b = ctx.enter_context(nc.psum_tensor("src_b", [P, H * P], F32))
        got = ctx.enter_context(nc.psum_tensor("got", [P, 2, 512], F32))
        added = ctx.enter_context(nc.psum_tensor("added", [P, 2, 512], F32))

        tables_made = sem("l0_tables_made")
        win_in = [sem(f"win_in{i}") for i in range(2)]
        win_split = sem("win_split")
        ids_shown = sem("ids_shown")
        onehot_made = sem("onehot_made")
        same_made = sem("same_made")
        fetched = sem("fetched")
        msgs_made = sem("msgs_made")
        summed = sem("summed")
        sums_out = sem("sums_out")
        rows_known = sem("rows_known")
        turns = sem("turns")
        table_add = g.table_add
        adds_ended = sem("adds_ended")
        msg_init = sem("msg_init")
        dve_step = sem("l0_dve_step")
        part_made = sem("part_made")
        row_step = sem("row_step")
        weights_in = sem("weights_in")
        windows_asked = sem("windows_asked")
        l1_step = sem("l1_step")
        block = ctx.enter_context(nc.Block())

        def passes(eng):
            return eng.Fori(0, eng.value_load(g.n_pass[0:1, 0:1], min_val=1, max_val=g.PASSES0))

        @block.sync
        def _(sp):
            sp.sem_inc(win_split, 2)
            w0, w1, w2, w3, w4 = [w.rearrange("u v w -> (u v) w") for w in w_tp]
            loads = [(w_scalar, w0, w3), (w_vec[0], w1, w2), (w_vec[1], w1, w4)]
            with passes(sp) as w:
                with sp.Fori(0, RN) as r:
                    sp.wait_ge(tables_made, w + 1)
                    for h in range(2):
                        n = (w * RN + r) * 2 + h
                        first_node = sp.value_load(start_i[0:1, bass.ds(r * 2 + h, 1)], min_val=0,
                                                   max_val=g.N - WIN0)
                        sp.wait_ge(win_split, n + 1)
                        sp.dma_start(win_x[h][:], x[bass.ds(first_node, WIN0), :]).then_inc(win_in[h], 16)
                    sp.sem_inc(windows_asked, 1)
            for to, from_scalars, from_vectors in loads:
                sp.dma_start(to[0:MUL, :], from_scalars).then_inc(weights_in, 16)
                for i in range(3):
                    sp.dma_start(to[MUL + i:P:3, :], from_vectors).then_inc(weights_in, 16)

        @block.tensor
        def _(pe):
            def show_ids(n, r, h):
                pe.wait_ge(same_made, n + 1)
                pick = g.ident_bf[0:RN, bass.ds(r, 1)].to_broadcast([RN, P])
                for to, parts in ((dst_b, g.hi_lo[1]), (src_b, g.hi_lo[0])):
                    for c in range(2):
                        cols = slice((2 * h + c) * 512, (2 * h + c + 1) * 512)
                        for k in range(2):
                            last = nc.tensor.matmul(to[:, c * 512:(c + 1) * 512], pick, parts[k][0:RN, cols],
                                                    start=(k == 0), stop=(k == 1))
                last.then_inc(ids_shown, 1)

            pe.sem_inc(same_made, 1)
            pe.sem_inc(msgs_made, 2)
            pe.sem_inc(sums_out, 2)
            pe.wait_ge(msg_init, 1)
            show_ids(0, 0, 0)
            with passes(pe) as w:
                with pe.Fori(0, RN) as r:
                    for h in range(2):
                        n = (w * RN + r) * 2 + h
                        pe.wait_ge(onehot_made, n + 1)
                        for q in range(2):
                            pe.wait_ge(msgs_made, n * 2 + q + 1)
                            for t in range(4 * q, 4 * q + 4):
                                for k in range(3):
                                    last = nc.tensor.matmul(got[:, q, (t % 4) * P:(t % 4 + 1) * P],
                                                            onehot[h][:, t * P:(t + 1) * P], win_s[h][:, k, :],
                                                            start=(k == 0), stop=(k == 2))
                            last.then_inc(fetched, 1)
                        show_ids(n + 1, r + h, 1 - h)
                        for j in range(4):
                            pe.wait_ge(msgs_made, n * 2 + j // 2 + 3)
                            pe.wait_ge(sums_out, n * 4 + j + 1)
                            for i in range(2):
                                t = 2 * j + i
                                last = nc.tensor.matmul(added[:, j % 2, i * R_COLS:(i + 1) * R_COLS],
                                                        same[h][:, t, :], msg[h][:, t, :], start=True, stop=True)
                            last.then_inc(summed, 1)

        @block.scalar
        def _(act):
            with passes(act) as w:
                with act.Fori(0, RN) as r:
                    for h in range(2):
                        n = (w * RN + r) * 2 + h
                        for q in range(2):
                            act.wait_ge(fetched, n * 2 + q + 1)
                            for t in range(4 * q, 4 * q + 4):
                                last = nc.scalar.activation(msg[h][:, t, 0:D], got[:, q, (t % 4) * P:(t % 4 + 1) * P],
                                                            ACT.Copy,
                                                            scale=g.w_col[:, bass.ds(r * ROW_TILES + (h * H + t), 1)])
                            last.then_inc(msgs_made, 1)
                        for j in range(4):
                            act.wait_ge(summed, n * 4 + j + 1)
                            act.wait_ge(turns, n * H + 2 * j + 2)
                            nc.scalar.copy(sums[:, h * H + 2 * j:h * H + 2 * j + 2, :],
                                           added[:, j % 2, 0:2 * R_COLS].rearrange("p (t c) -> p t c", t=2)
                                           ).then_inc(sums_out, 1)

        @block.vector
        def _(dve):
            for h in range(2):
                last = nc.vector.tensor_copy(msg[h][:, :, D:R_COLS],
                                             g.cst[:, C_DUPW:C_DUPW + 2].unsqueeze(1).to_broadcast([P, H, 2]))
            last.then_inc(msg_init, 1)
            halves = g.half_start[:].rearrange("p r h -> p (r h)")
            pid = g.cst[:, C_PID:C_PID + 1]
            spare = g.cst[:, C_SPARE:C_SPARE + 1]
            nc.vector.memset(moved[:, 0:1], 0.0).then_inc(dve_step, 1)
            nc.vector.tensor_copy(moved[:, 1:2], pid).then_inc(dve_step, 1)

            def half(u, r, h):
                n = u * 2 + h
                own = bass.ds(r * 2 + h, 1)
                cols = bass.ds(r * ROW_TILES + h * H, H)
                dve.wait_ge(win_in[h], u * 16 + 16)
                dve.wait_ge(ids_shown, n + 1)
                nc.vector.tensor_copy(win_s[h][:, 0, :], win_x[h][:]).then_inc(part_made, 1)
                dve.wait_ge(part_made, n * 3 + 1)
                nc.vector.tensor_tensor(win_r[h][:], win_x[h][:], win_s[h][:, 0, :],
                                        ALU.subtract).then_inc(win_split, 1)
                dve.wait_ge(win_split, n + 3)
                nc.vector.tensor_copy(win_s[h][:, 1, :], win_r[h][:]).then_inc(part_made, 1)
                dve.wait_ge(part_made, n * 3 + 2)
                nc.vector.tensor_tensor(win_s[h][:, 2, :], win_r[h][:], win_s[h][:, 1, :],
                                        ALU.subtract).then_inc(part_made, 1)
                nc.vector.tensor_scalar(onehot[h][:], dst_b[:], node_id[:, own], None,
                                        ALU.is_equal).then_inc(onehot_made, 1)
                nc.vector.tensor_tensor(same[h][:], src_b[:].rearrange("p (t e) -> p t e", t=H),
                                        g.src_col[:, cols].unsqueeze(2).to_broadcast([P, H, P]),
                                        ALU.is_equal).then_inc(same_made, 1)

            def rows_of(u, r, h):
                n = u * 2 + h
                cols = bass.ds(r * ROW_TILES + h * H, H)
                own = slice(h * H, (h + 1) * H)
                dve.wait_ge(sums_out, n * 4 + 6)
                dve.wait_ge(rows_known, n + 1)
                nc.vector.tensor_scalar(away[:], g.src_col[:, cols], spare, None, ALU.subtract).then_inc(row_step, 1)
                nc.vector.tensor_tensor(first2[:], sums[:, own, D:R_COLS],
                                        g.cst[:, C_DUPT:C_DUPT + 2].unsqueeze(1).to_broadcast([P, H, 2]),
                                        ALU.is_lt).then_inc(row_step, 1)
                dve.wait_ge(row_step, n * 4 + 2)
                nc.vector.tensor_tensor(first[:], first2[:, :, 0], first2[:, :, 1], ALU.mult).then_inc(row_step, 1)
                dve.wait_ge(row_step, n * 4 + 3)
                nc.vector.tensor_tensor(away[:], away[:], first[:], ALU.mult).then_inc(row_step, 1)
                dve.wait_ge(row_step, n * 4 + 4)
                dve.wait_ge(turns, n * H + H)
                nc.vector.tensor_scalar(row_no[:, own], away[:], spare, None, ALU.add).then_inc(rows_known, 1)

            def layer1_tables(dve):
                TN, Q, R = g.TN, QUAD_TILES, ROW_TILES
                steps = [0]

                def link(ins):
                    steps[0] += 1
                    ins.then_inc(l1_step, 1)
                    dve.wait_ge(l1_step, steps[0])

                coef = g.cst[:, C_COEF:C_COEF + 4 * NA].rearrange("p (m c) -> p m c", c=4)
                dve.wait_ge(weights_in, 16 * 12)
                nc.vector.tensor_tensor(g.mix[:, :, 0:MUL], w_scalar[:].unsqueeze(1).to_broadcast([P, NA, MUL]),
                                        coef[:, :, 0:1].to_broadcast([P, NA, MUL]), ALU.mult)
                vec = g.mix[:, :, MUL:D].rearrange("p m (w k) -> p m w k", k=3)
                for wv, m0, m1 in ((w_vec[0], 0, 4), (w_vec[1], 4, NA)):
                    s4 = [P, m1 - m0, MUL, 3]
                    nc.vector.tensor_tensor(vec[:, m0:m1], wv[:].unsqueeze(1).unsqueeze(3).to_broadcast(s4),
                                            coef[:, m0:m1, 1:4].unsqueeze(2).to_broadcast(s4), ALU.mult)
                keep = g.keep[:, 1:2]
                starts = g.tile_start[:]
                by4 = starts.rearrange("p (a b) -> p a b", b=Q)
                off4 = off_f[:].rearrange("p (a b) -> p a b", b=Q)
                quad_first = starts.rearrange("p (a b c) -> p a b c", b=R // Q, c=Q)[:, :, :, 0]
                offq = off_f[:, 0:TN // Q].rearrange("p (a b) -> p a b", b=R // Q)

                def pack(offs, words, bits, out):
                    shift = float(2 ** bits)
                    link(nc.vector.scalar_tensor_tensor(words, offs[:, :, 3], shift, offs[:, :, 2], ALU.mult, ALU.add))
                    link(nc.vector.scalar_tensor_tensor(words, words, shift, offs[:, :, 1], ALU.mult, ALU.add))
                    link(nc.vector.tensor_scalar(out, words, keep, None, ALU.mult))

                assert 2 ** TILE_BITS > QUAD_WIN - WIN and 2 ** QUAD_BITS > GROUP_WIN - QUAD_WIN
                assert 3 * QUAD_BITS <= 24
                link(nc.vector.tensor_tensor(off4[:, :, 1:Q], by4[:, :, 1:Q],
                                             by4[:, :, 0:1].to_broadcast([P, TN // Q, Q - 1]), ALU.subtract))
                pack(off4, word_f[:], TILE_BITS, g.tile_offs[:])
                link(nc.vector.tensor_tensor(offq, quad_first, quad_first[:, :, 0:1].to_broadcast([P, RN, R // Q]),
                                             ALU.subtract))
                pack(offq, word_f[:, 0:RN], QUAD_BITS, g.quad_offs[:])
                link(nc.vector.tensor_scalar(off_f[:], starts, keep, None, ALU.mult))
                nc.vector.tensor_tensor(g.dst_rel[:], g.dst_col[:], off_f[:], ALU.subtract)
                link(nc.vector.tensor_copy(g.row_f[:], off_f[:].rearrange("p (a b) -> p a b", b=R)[:, :, 0]))
                link(nc.vector.tensor_copy(g.row_start[:], g.row_f[:]))

            dve.sem_inc(rows_known, 1)
            with passes(dve) as w:
                dve.wait_ge(dve_step, w * 4 + 2)
                nc.vector.tensor_scalar(node_id[:], halves, g.keep[:, 0:1], moved[:, 1:2], ALU.mult,
                                        ALU.add).then_inc(dve_step, 1)
                nc.vector.tensor_scalar(start_i[:], halves, g.keep[:, 0:1], moved[:, 0:1], ALU.mult,
                                        ALU.add).then_inc(tables_made, 1)
                dve.wait_ge(tables_made, w + 1)
                dve.wait_ge(dve_step, w * 4 + 3)
                nc.vector.tensor_scalar(moved[:], moved[:], g.jump[:, 0:1], None, ALU.add).then_inc(dve_step, 1)
                half(w * RN, 0, 0)
                half(w * RN, 0, 1)
                rows_of(w * RN, 0, 0)
                with dve.Fori(1, RN) as r:
                    half(w * RN + r, r, 0)
                    rows_of(w * RN + r - 1, r - 1, 1)
                    half(w * RN + r, r, 1)
                    rows_of(w * RN + r, r, 0)
                rows_of(w * RN + RN - 1, RN - 1, 1)
                dve.sem_inc(dve_step, 2)
            layer1_tables(dve)

        @block.gpsimd
        def _(pool):
            pool.wait_ge(windows_asked, 1)
            fill(pool, g, tables, TABLES - 1)
            pool.sem_inc(turns, 2 * H - TABLES)
            with passes(pool) as w:
                with pool.Fori(0, RN) as r:
                    for h in range(2):
                        n = (w * RN + r) * 2 + h
                        for t in range(H):
                            k = t % TABLES
                            use = n * (H // TABLES) + t // TABLES
                            if t == 0:
                                pool.wait_ge(rows_known, n + 2)
                            pool.wait_ge(table_add[k], use * 16 + 16)
                            pool.sem_inc(turns, 1)
                            pool.indirect_dma_start(
                                tables[k], bass.IndirectOffsetOnAxis(ap=row_no[:, h * H + t:h * H + t + 1], axis=0),
                                sums[:, h * H + t, 0:D], None, compute_op=ALU.add).then_inc(table_add[k], 16)
            passes_run = pool.value_load(g.n_pass[0:1, 0:1], min_val=1, max_val=g.PASSES0)
            for k in range(TABLES):
                pool.wait_ge(table_add[k], passes_run * (16 * RN * ROW_TILES // TABLES) + 16)
            pool.sem_inc(adds_ended, 1)


BATCH = 4
SLOTS = 4


def norm_stage(nc, g, name, x_in, x_out, tables):
    NB = g.N // (BATCH * P)
    assert NB % SLOTS == 0 and NB > SLOTS
    with ExitStack() as ctx:
        def sb(n, shape, dt):
            return ctx.enter_context(nc.sbuf_tensor(f"{name}_{n}", shape, dt))

        def sem(n):
            return ctx.enter_context(nc.semaphore(f"{name}_{n}"))

        n_in = 1 + (len(tables) if tables else 0)
        x_t = [sb(f"x{i}", [P, BATCH, D], F32) for i in range(SLOTS)]
        tab_t = [[sb(f"t{i}_{k}", [P, BATCH, D], F32) for k in range(n_in - 1)] for i in range(SLOTS)]
        z = [sb(f"z{i}", [P, BATCH, D], F32) for i in range(SLOTS)]
        feat = [sb(f"feat{i}", [P, BATCH, P], F32) for i in range(2)]
        stats = [sb(f"stats{i}", [P, BATCH, 6], F32) for i in range(2)]
        mv = [sb(f"mv{i}", [P, BATCH, 2], F32) for i in range(2)]
        var = [sb(f"var{i}", [P, BATCH], F32) for i in range(2)]
        std = [sb(f"std{i}", [P, BATCH], F32) for i in range(2)]
        rstd = [sb(f"rstd{i}", [P, BATCH], F32) for i in range(2)]
        shift = [sb(f"shift{i}", [P, BATCH], F32) for i in range(2)]
        pre = ctx.enter_context(nc.psum_tensor(f"{name}_pre", [P, 2, 512], F32))
        y = ctx.enter_context(nc.psum_tensor(f"{name}_y", [P, 2, 512], F32))

        loaded = [sem(f"loaded{i}") for i in range(SLOTS)]
        free = sem("free")
        tab_sum = sem("tab_sum")
        pool_step = sem("pool_step")
        pre_made = sem("pre_made")
        feat_made = sem("feat_made")
        y_made = sem("y_made")
        stat_step = sem("stat_step")
        aggr_turn = sem("aggr_turn")
        var_made = sem("var_made")
        std_made = sem("std_made")
        rstd_made = sem("rstd_made")
        shift_made = sem("shift_made")
        normed = sem("normed")
        stored = [sem(f"stored{i}") for i in range(SLOTS)]
        block = ctx.enter_context(nc.Block())

        def tiles(ap):
            return ap.rearrange("(b p a) d -> b p a d", p=P, a=BATCH)

        @block.sync
        def _(sp):
            sp.sem_inc(free, SLOTS)
            with sp.Fori(0, NB // SLOTS) as i:
                for s in range(SLOTS):
                    b = i * SLOTS + s
                    sp.wait_ge(free, b + 1)
                    for k in range(n_in - 1):
                        sp.dma_start(tab_t[s][k][:], tiles(tables[k][0:g.N, :])[bass.ds(b, 1)].squeeze(0)
                                     ).then_inc(loaded[s], 16)
                    sp.dma_start(x_t[s][:], tiles(x_in)[bass.ds(b, 1)].squeeze(0)).then_inc(loaded[s], 16)

        @block.gpsimd
        def _(pool):
            if tables:
                assert len(tables) == 4
                with pool.Fori(0, NB // SLOTS) as i:
                    for s in range(SLOTS):
                        t0, t1, t2, t3 = [t[:] for t in tab_t[s]]
                        pool.wait_ge(loaded[s], i * (16 * n_in) + 16 * n_in)
                        nc.gpsimd.tensor_tensor(t0, t0, t1, ALU.add).then_inc(pool_step, 1)
                        nc.gpsimd.tensor_tensor(t2, t2, t3, ALU.add).then_inc(pool_step, 1)
                        pool.wait_ge(pool_step, i * (2 * SLOTS) + (2 * s + 2))
                        nc.gpsimd.tensor_tensor(t0, t0, t2, ALU.add).then_inc(tab_sum, 1)
            else:
                pool.sem_inc(y_made, 2)
                with pool.Fori(0, NB // 2) as i:
                    for s in range(2):
                        b = i * 2 + s
                        pool.wait_ge(y_made, b + 1)
                        nc.gpsimd.tensor_copy(feat[s][:], g.acc[:, bass.ds(b * (BATCH * P), BATCH * P)].rearrange(
                            "f (p a) -> f a p", a=BATCH)).then_inc(feat_made, 1)

        @block.tensor
        def _(pe):
            ident = g.cst[:, C_IDENT:C_IDENT + P]
            if tables:
                pe.sem_inc(feat_made, 2)
            with pe.Fori(0, NB // SLOTS) as i:
                for s in range(SLOTS):
                    b = i * SLOTS + s
                    if tables:
                        pe.wait_ge(tab_sum, b + 1)
                        pe.wait_ge(feat_made, b + 1)
                        for a in range(BATCH):
                            last = nc.tensor.transpose(pre[:, s % 2, a * P:(a + 1) * P], tab_t[s][0][:, a, :], ident)
                        last.then_inc(pre_made, 1)
                        pe.wait_ge(feat_made, b + 3)
                        pe.wait_ge(free, b + (SLOTS - 1))
                        for a in range(BATCH):
                            last = nc.tensor.matmul(y[:, s % 2, a * P:(a + 1) * P], feat[s % 2][:, a, :], g.w_t[:],
                                                    start=True, stop=True)
                        last.then_inc(y_made, 1)
                    else:
                        pe.wait_ge(feat_made, b + 1)
                        pe.wait_ge(free, b + (SLOTS - 1))
                        for a in range(BATCH):
                            last = nc.tensor.transpose(y[:, s % 2, a * P:(a + 1) * P], feat[s % 2][:, a, :], ident)
                        last.then_inc(y_made, 1)

        @block.scalar
        def _(act):
            def features(b, s):
                if tables:
                    act.wait_ge(pre_made, b + 1)
                    nc.scalar.copy(feat[s % 2][:].rearrange("p a n -> p (a n)"), pre[:, s % 2, :]
                                   ).then_inc(feat_made, 1)

            def root(b, s):
                act.wait_ge(var_made, b + 1)
                nc.scalar.activation(std[s % 2][:], var[s % 2][:], ACT.Sqrt).then_inc(std_made, 1)

            def norm(b, s):
                act.wait_ge(shift_made, b + 1)
                for a in range(BATCH):
                    last = nc.scalar.activation(z[s][:, a, :], z[s][:, a, :], ACT.Identity,
                                                bias=shift[s % 2][:, a:a + 1], scale=rstd[s % 2][:, a:a + 1])
                last.then_inc(normed, 1)

            def store(b, s):
                act.wait_ge(normed, b + 1)
                act.dma_start(tiles(x_out)[bass.ds(b, 1)].squeeze(0), z[s][:]).then_inc(stored[s], 16)

            for s in range(SLOTS):
                features(s, s)
                if s >= 1:
                    root(s - 1, s - 1)
                if s >= 2:
                    norm(s - 2, s - 2)
                    store(s - 2, s - 2)
            with act.Fori(1, NB // SLOTS) as i:
                for s in range(SLOTS):
                    features(i * SLOTS + s, s)
                    root(i * SLOTS + (s - 1), (s - 1) % SLOTS)
                    norm(i * SLOTS + (s - 2), (s - 2) % SLOTS)
                    store(i * SLOTS + (s - 2), (s - 2) % SLOTS)
            root(NB - 1, SLOTS - 1)
            for s in (SLOTS - 2, SLOTS - 1):
                norm(NB - SLOTS + s, s)
                store(NB - SLOTS + s, s)
            for s in range(SLOTS):
                act.wait_ge(stored[s], 16 * (NB // SLOTS))

        @block.vector
        def _(dve):
            y_credit = 0 if tables else 2

            def measure(i, s, first):
                b = i * SLOTS + s
                dve.wait_ge(y_made, b + (1 + y_credit))
                dve.wait_ge(loaded[s], i * (16 * n_in) + 16 * n_in)
                if not first:
                    dve.wait_ge(stored[s], i * 16)
                nc.vector.tensor_tensor(z[s][:], x_t[s][:], y[:, s % 2, :].rearrange("p (a d) -> p a d", a=BATCH),
                                        ALU.add).then_inc(free, 1)
                dve.wait_ge(free, b + (SLOTS + 1))
                for a in range(BATCH):
                    nc.vector.bn_stats(stats[s % 2][:, a, :], z[s][:, a, :]).then_inc(stat_step, 1)
                dve.wait_ge(stat_step, b * 8 + 4)
                if not first or s >= 2:
                    dve.wait_ge(shift_made, b - 1)
                dve.sem_inc(aggr_turn, 1)
                for a in range(BATCH):
                    nc.vector.bn_aggr(mv[s % 2][:, a, :], stats[s % 2][:, a, :]).then_inc(stat_step, 1)
                dve.wait_ge(stat_step, b * 8 + 8)
                nc.vector.tensor_scalar(var[s % 2][:], mv[s % 2][:, :, 1], EPS, None, ALU.add).then_inc(var_made, 1)

            def scale(b, s, first):
                dve.wait_ge(std_made, b + 1)
                if not first:
                    dve.wait_ge(normed, b - 1)
                nc.vector.reciprocal(rstd[s % 2][:], std[s % 2][:]).then_inc(rstd_made, 1)
                dve.wait_ge(rstd_made, b + 1)
                nc.vector.scalar_tensor_tensor(shift[s % 2][:], mv[s % 2][:, :, 0], -1.0, rstd[s % 2][:],
                                               ALU.mult, ALU.mult).then_inc(shift_made, 1)

            for s in range(SLOTS):
                measure(0, s, True)
                if s >= 1:
                    scale(s - 1, s - 1, s < 3)
            with dve.Fori(1, NB // SLOTS) as i:
                for s in range(SLOTS):
                    measure(i, s, False)
                    scale(i * SLOTS + (s - 1), (s - 1) % SLOTS, False)
            scale(NB - 1, SLOTS - 1, False)


def offset_in(word, k, bits, most):
    if k == 0:
        return 0
    low = (word >> (bits * (k - 1))) if k > 1 else word
    return (low & (2 ** bits - 1)).with_bounds(min_val=0, max_val=most)


def layer1(nc, g, x1, attr):
    RN, TN = g.RN, g.TN
    H, Q, R = HALF_TILES, QUAD_TILES, ROW_TILES
    with ExitStack() as ctx:
        def sb(name, shape, dt):
            return ctx.enter_context(nc.sbuf_tensor(name, shape, dt))

        def sem(name):
            return ctx.enter_context(nc.semaphore(name))

        zero_bf = sb("zero_bf", [P, NA * QUAD_WIN], BF16)
        ids = [sb(f"ids{h}", [P, H], I32) for h in range(2)]
        feat = sb("feat", [P, R, D], F32)
        attr_in = [sb(f"attr_in{z}", [R, P * NA], F32) for z in range(2)]
        hot = sb("hot", [P, H, WIN], F32)
        attr_hot = [sb(f"attr_hot{h}", [P, H, NA, WIN], F32) for h in range(2)]
        group = [sb(f"group{z}", [P, NA, GROUP_WIN], F32) for z in range(2)]
        quad = ctx.enter_context(nc.psum_tensor("quad", [P, Q, 512], F32))
        attr_t = ctx.enter_context(nc.psum_tensor("attr_t", [P, 2, 512], F32))
        mixed = ctx.enter_context(nc.psum_tensor("mixed", [P, 2, 512], F32))

        zero_made = sem("zero_made")
        move_step = sem("move_step")
        ids_made = sem("ids_made")
        feat_in = [sem(f"feat_in{t}") for t in range(R)]
        attr_here = [sem(f"attr_here{z}") for z in range(2)]
        attr_turned = sem("attr_turned")
        feat_used = sem("feat_used")
        hot_step = sem("hot_step")
        hot_made = sem("hot_made")
        quad_added = sem("quad_added")
        group_zero = sem("group_zero")
        group_used = sem("group_used")
        acc_added = sem("acc_added")
        pool_turn = sem("pool_turn")
        pe_turn = sem("pe_turn")
        dve_turn = sem("dve_turn")
        loads_ended = sem("loads_ended")
        block = ctx.enter_context(nc.Block())

        def passes(eng):
            return eng.Fori(0, eng.value_load(g.n_pass[0:1, 1:2], min_val=1, max_val=g.PASSES1))

        @block.sync
        def _(sp):
            attr_rows = attr.rearrange("(r t e) m -> r t (e m)", t=R, e=P)

            def load_attr(v, row, z):
                sp.wait_ge(attr_turned, v + 1)
                sp.dma_start(attr_in[z][:], attr_rows[bass.ds(row, 1)].squeeze(0)).then_inc(attr_here[z], 16)

            sp.sem_inc(attr_turned, 2)
            load_attr(0, 0, 0)
            with passes(sp) as w:
                with sp.Fori(0, RN // 2 - 1) as i:
                    load_attr(w * RN + i * 2 + 1, i * 2 + 1, 1)
                    load_attr(w * RN + i * 2 + 2, i * 2 + 2, 0)
                load_attr(w * RN + RN - 1, RN - 1, 1)
                load_attr(w * RN + RN, 0, 0)
            n_loads = sp.value_load(g.n_pass[0:1, 1:2], min_val=1, max_val=g.PASSES1)
            for z in range(2):
                sp.wait_ge(attr_here[z], n_loads * (8 * RN) + 16 * (1 - z))
            sp.sem_inc(loads_ended, 1)

        @block.gpsimd
        def _(pool):
            with passes(pool) as w:
                with pool.Fori(0, RN) as r:
                    u = w * RN + r
                    for q in range(R // Q):
                        if q % 2 == 0:
                            pool.wait_ge(ids_made, u * 2 + (q // 2 + 1))
                        pool.wait_ge(feat_used, u * R + 4 * q + 4)
                        pool.sem_inc(pool_turn, 1)
                        for t in range(Q * q, Q * q + Q):
                            pool.indirect_dma_start(
                                feat[:, t, :], None, x1,
                                bass.IndirectOffsetOnAxis(ap=ids[t // H][:, t % H:t % H + 1], axis=0),
                            ).then_inc(feat_in[t], 16)
            passes_run = pool.value_load(g.n_pass[0:1, 1:2], min_val=1, max_val=g.PASSES1)
            for t in range(R):
                pool.wait_ge(feat_in[t], passes_run * (16 * RN))
            pool.sem_inc(pool_turn, 1)

        @block.scalar
        def _(act):
            act.sem_inc(group_used, 2)
            for h in range(2):
                nc.scalar.copy(ids[h][:], g.src_col[:, h * H:h * H + H]).then_inc(ids_made, 1)
            with passes(act) as w:
                with act.Fori(0, RN // 2) as i:
                    for z in range(2):
                        r = i * 2 + z
                        u = w * RN + r
                        act.wait_ge(group_used, u + 1)
                        nc.scalar.memzero(group[z][:]).then_inc(group_zero, 1)
                        for h in range(2):
                            for t in range(h * H, h * H + H):
                                act.wait_ge(feat_in[t], u * 16 + 16)
                            nc.scalar.copy(ids[h][:], g.src_col[:, bass.ds(r * R + (R + h * H), H)]
                                           ).then_inc(ids_made, 1)

        @block.tensor
        def _(pe):
            pe.sem_inc(feat_used, R)
            pe.sem_inc(quad_added, R // Q)
            pe.sem_inc(acc_added, 2)

            def turn_attr(v, v_half, z):
                pe.wait_ge(attr_here[z], v_half * 16 + 16)
                pe.wait_ge(hot_made, v * 2 + 1)
                pe.sem_inc(pe_turn, 1)
                edges = attr_in[z][:].rearrange("t (e m) -> t e m", m=NA)
                for m in range(NA):
                    last = nc.tensor.transpose(attr_t[:, z, m * R:(m + 1) * R], edges[:, :, m],
                                               g.cst[0:R, C_IDENT:C_IDENT + R])
                last.then_inc(attr_turned, 1)

            turn_attr(0, 0, 0)
            pe.wait_ge(zero_made, 1)
            with passes(pe) as w:
                with pe.Fori(0, RN // 2) as i:
                    for z in range(2):
                        r = i * 2 + z
                        u = w * RN + r
                        for q in range(R // Q):
                            word = pe.value_load(g.tile_offs[0:1, bass.ds(r * (R // Q) + q, 1)], min_val=0,
                                                 max_val=2 ** (3 * TILE_BITS) - 1)
                            pe.wait_ge(quad_added, u * 4 + q + 1)
                            nc.tensor.matmul(quad[:, q, 0:NA * QUAD_WIN], zero_bf[0:1, 0:P], zero_bf[0:1, :],
                                             start=True, stop=False, skip_group_check=True)
                            if q % 2 == 0:
                                pe.wait_ge(hot_made, u * 2 + (q // 2 + 4))
                            bank = quad[:, q, 0:NA * QUAD_WIN].rearrange("p (m n) -> p m n", m=NA)
                            for t in range(Q * q, Q * q + Q):
                                off = offset_in(word, t % Q, TILE_BITS, QUAD_WIN - WIN)
                                pe.wait_ge(feat_in[t], u * 16 + 16)
                                nc.tensor.matmul(bank[:, :, bass.ds(off, WIN)], feat[:, t, :],
                                                 attr_hot[t // H][:, t % H, :, :], start=False,
                                                 stop=(t % Q == Q - 1), skip_group_check=True
                                                 ).then_inc(feat_used, 1)
                        turn_attr(u + 1, w * (RN // 2) + i + z, 1 - z)
                        pe.wait_ge(quad_added, u * 4 + 8)
                        pe.wait_ge(acc_added, u + 1)
                        for m in range(NA):
                            last = nc.tensor.matmul(mixed[:, z, 0:GROUP_WIN], g.mix[:, m, :], group[z][:, m, :],
                                                    start=(m == 0), stop=(m == NA - 1))
                        last.then_inc(group_used, 1)

        @block.vector
        def _(dve):
            nc.vector.memset(zero_bf[:], 0.0).then_inc(zero_made, 1)
            dve.sem_inc(hot_made, 3)

            def hots(u, r, h, z):
                cols = bass.ds(r * R + h * H, H)
                s3, s4 = [P, H, WIN], [P, H, NA, WIN]
                by_tile = attr_t[:, z, 0:NA * R].rearrange("p (m t) -> p t m", m=NA)
                dve.wait_ge(hot_made, u * 2 + (h + 3))
                nc.vector.tensor_tensor(hot[:], g.cst[:, C_IOTA:C_IOTA + WIN].unsqueeze(1).to_broadcast(s3),
                                        g.dst_rel[:, cols].unsqueeze(2).to_broadcast(s3),
                                        ALU.is_equal).then_inc(hot_step, 1)
                dve.wait_ge(hot_step, u * 2 + (h + 1))
                dve.wait_ge(attr_turned, u + 3)
                dve.wait_ge(feat_used, u * R + (h * H + H))
                nc.vector.tensor_tensor(attr_hot[h][:], hot[:].unsqueeze(2).to_broadcast(s4),
                                        by_tile[:, h * H:h * H + H, :].unsqueeze(3).to_broadcast(s4),
                                        ALU.mult).then_inc(hot_made, 1)

            def add_quads(u, r, z):
                word = dve.value_load(g.quad_offs[0:1, bass.ds(r, 1)], min_val=0, max_val=2 ** (3 * QUAD_BITS) - 1)
                for q in range(R // Q):
                    off = offset_in(word, q, QUAD_BITS, GROUP_WIN - QUAD_WIN)
                    if q:
                        dve.wait_ge(quad_added, u * 4 + (q + 4))
                    else:
                        dve.wait_ge(group_zero, u + 1)
                    dve.wait_ge(feat_used, u * R + (R + 4 * q + 4))
                    to = group[z][:, :, bass.ds(off, QUAD_WIN)]
                    nc.vector.tensor_tensor(to, to, quad[:, q, 0:NA * QUAD_WIN].rearrange("p (m n) -> p m n", m=NA),
                                            ALU.add).then_inc(quad_added, 1)

            def add_row(u, r, z):
                at = dve.value_load(g.row_start[0:1, bass.ds(r, 1)], min_val=0, max_val=g.N - 1)
                dve.wait_ge(group_used, u + 3)
                dve.wait_ge(acc_added, u + 2)
                to = g.acc[:, bass.ds(at, GROUP_WIN)]
                nc.vector.tensor_tensor(to, to, mixed[:, z, 0:GROUP_WIN], ALU.add).then_inc(acc_added, 1)

            with passes(dve) as w:
                def row_pair(i, first):
                    for z in range(2):
                        r = i * 2 + z
                        u = w * RN + r
                        hots(u, r, 0, z)
                        if z or not first:
                            add_row(u - 1, r - 1, 1 - z)
                        hots(u, r, 1, z)
                        add_quads(u, r, z)

                row_pair(0, True)
                with dve.Fori(1, RN // 2) as i:
                    row_pair(i, False)
                jump = g.jump[:, 1:2]
                nc.vector.tensor_scalar(g.dst_rel[:], g.dst_rel[:], jump, None, ALU.subtract).then_inc(move_step, 1)
                nc.vector.tensor_scalar(g.row_f[:], g.row_f[:], jump, None, ALU.add).then_inc(move_step, 1)
                add_row(w * RN + RN - 1, RN - 1, 1)
                dve.wait_ge(move_step, w * 3 + 2)
                nc.vector.tensor_copy(g.row_start[:], g.row_f[:]).then_inc(move_step, 1)
                dve.wait_ge(move_step, w * 3 + 3)
                dve.sem_inc(dve_turn, 1)


_INS = ["x", "src", "dst", "edge_attr_9", "edge_weight", "L0_gnn_W"] + [f"L1_gnn_w{k}" for k in range(5)]


def kernel(**inputs):
    import concourse.bacc as _bacc
    from concourse.bass_utils import run_bass_kernel_spmd as _run

    nc = _bacc.Bacc("TRN2", target_bir_lowering=False, num_devices=1)
    arrays, args = {}, []
    for name in _INS + ["constants"]:
        a = np.ascontiguousarray(inputs[name] if name in inputs else constants(inputs["x"].shape[0]))
        arrays[f"in_{name}"] = a
        args.append(nc.dram_tensor(f"in_{name}", a.shape, mybir.dt.from_np(a.dtype), kind="ExternalInput").ap())
    n = inputs["x"].shape[0]
    out = nc.dram_tensor("out_0", (n, D), F32, kind="ExternalOutput").ap()
    tables = [nc.dram_tensor(f"table{k}", (n + P, D), F32, kind="Internal").ap() for k in range(TABLES)]
    x1 = nc.dram_tensor("x1", (n, D), F32, kind="Internal").ap()
    x, src, dst, attr, weight, w_lin, *w_tp, consts = args
    gnn_kernel(nc, x, src, dst, attr, weight, w_lin, w_tp, consts, out, tables, x1)
    return _run(nc, [arrays], core_ids=[0]).results[0]["out_0"]
```
